# Optimizing a Trainium2 kernel written in Bass

```python
import numpy as np
import jax
import jax.numpy as jnp

def _softmax(x, axis=-1):
    return jax.nn.softmax(x, axis=axis)

def _gelu(x):
    return jax.nn.gelu(x, approximate=True)

def _silu(x):
    return jax.nn.silu(x)

def _sigmoid(x):
    return jax.nn.sigmoid(x)

def _layernorm(x, axis=-1, eps=1e-05):
    m = jnp.mean(x, axis=axis, keepdims=True)
    v = jnp.var(x, axis=axis, keepdims=True)
    return (x - m) / jnp.sqrt(v + eps)

def _scatter_add(tgt, idx, src, axis=0):
    return tgt.at[idx].add(src)

def _segment_sum(src, seg, n):
    return jax.ops.segment_sum(src, seg, n)
kernel_name = 'mk_hybrid_d1_jaxref_r8_0b01ab'

def setup_inputs(seed: int=0):
    np.random.seed(seed)
    _w = jnp.asarray

    def _L0_attn_a_setup():
        import jax, jax.numpy as jnp
        import numpy as np
        B, N, D = (2, 1024, 128)
        H = 16
        HD = D // H
        EPS = 1e-06

        def _feature_map(a):
            return jax.nn.elu(a) + 1.0
        key = jax.random.key(seed)
        ks = jax.random.split(key, 5)
        scale = 1.0 / np.sqrt(D)
        return {'x': jax.random.normal(ks[0], (B, N, D), dtype=jnp.float32), 'Wq': jax.random.normal(ks[1], (D, D), dtype=jnp.float32) * scale, 'Wk': jax.random.normal(ks[2], (D, D), dtype=jnp.float32) * scale, 'Wv': jax.random.normal(ks[3], (D, D), dtype=jnp.float32) * scale, 'Wo': jax.random.normal(ks[4], (D, D), dtype=jnp.float32) * scale}
    _L0_attn_a_in = _L0_attn_a_setup()

    def _L0_attn_b_setup():
        import jax, jax.numpy as jnp
        import numpy as np
        import math
        CHUNK = 128
        key = jax.random.key(seed)
        ks = jax.random.split(key, 12)
        B, S, H, D = (2, 512, 128, 256)
        std = 0.02
        inp = {'hidden_states': jax.random.normal(ks[0], (B, S, H), jnp.float32), 'Wq': jax.random.normal(ks[1], (H, D), jnp.float32) * std, 'bq': jnp.zeros((D,), jnp.float32), 'Wk': jax.random.normal(ks[2], (H, D), jnp.float32) * std, 'bk': jnp.zeros((D,), jnp.float32), 'Wv': jax.random.normal(ks[3], (H, D), jnp.float32) * std, 'bv': jnp.zeros((D,), jnp.float32), 'Wg': jax.random.normal(ks[4], (H, D), jnp.float32) * std, 'bg': jnp.zeros((D,), jnp.float32), 'Wo': jax.random.normal(ks[5], (D, H), jnp.float32) * std, 'bo': jnp.zeros((H,), jnp.float32)}
        return inp
    _L0_attn_b_in = _L0_attn_b_setup()

    def _L0_ffn_setup():
        import jax, jax.numpy as jnp
        import numpy as np
        D_MODEL = 128
        D_OUT = 128
        RANK = 16
        NUM_TRUE = 8
        NUM_NULL = 2
        TOP_K = 2
        SCALING = 32.0 / 16.0
        key = jax.random.key(seed)
        ks = jax.random.split(key, 6)
        x = jax.random.normal(ks[0], (4, 512, D_MODEL), dtype=jnp.float32)
        base_w = jax.random.normal(ks[1], (D_OUT, D_MODEL), dtype=jnp.float32) / np.sqrt(D_MODEL)
        base_b = jax.random.normal(ks[2], (D_OUT,), dtype=jnp.float32) * 0.01
        gate_w = jax.random.normal(ks[3], (NUM_TRUE + NUM_NULL, D_MODEL), dtype=jnp.float32) / np.sqrt(D_MODEL)
        lora_A = jax.random.normal(ks[4], (NUM_TRUE, RANK, D_MODEL), dtype=jnp.float32) / np.sqrt(D_MODEL)
        lora_B = jax.random.normal(ks[5], (NUM_TRUE, D_OUT, RANK), dtype=jnp.float32) * 0.01
        return {'x': x, 'base_w': base_w, 'base_b': base_b, 'gate_w': gate_w, 'lora_A': lora_A, 'lora_B': lora_B}
    _L0_ffn_in = _L0_ffn_setup()
    _d = {'L0_attn_a_x': _L0_attn_a_in['x'], 'L0_attn_a_Wq': _L0_attn_a_in['Wq'], 'L0_attn_a_Wk': _L0_attn_a_in['Wk'], 'L0_attn_a_Wv': _L0_attn_a_in['Wv'], 'L0_attn_a_Wo': _L0_attn_a_in['Wo'], 'L0_attn_b_Wq': _L0_attn_b_in['Wq'], 'L0_attn_b_bq': _L0_attn_b_in['bq'], 'L0_attn_b_Wk': _L0_attn_b_in['Wk'], 'L0_attn_b_bk': _L0_attn_b_in['bk'], 'L0_attn_b_Wv': _L0_attn_b_in['Wv'], 'L0_attn_b_bv': _L0_attn_b_in['bv'], 'L0_attn_b_Wg': _L0_attn_b_in['Wg'], 'L0_attn_b_bg': _L0_attn_b_in['bg'], 'L0_attn_b_Wo': _L0_attn_b_in['Wo'], 'L0_attn_b_bo': _L0_attn_b_in['bo'], 'L0_ffn_base_w': _L0_ffn_in['base_w'], 'L0_ffn_base_b': _L0_ffn_in['base_b'], 'L0_ffn_gate_w': _L0_ffn_in['gate_w'], 'L0_ffn_lora_A': _L0_ffn_in['lora_A'], 'L0_ffn_lora_B': _L0_ffn_in['lora_B']}
    _x0 = _d['L0_attn_a_x']
    _d['L0_attn_a_x'] = jax.random.normal(jax.random.fold_in(jax.random.key(seed), 1), (2, 1024, 128), dtype=_x0.dtype)
    del _x0
    return _d

def reference(L0_attn_a_x, L0_attn_a_Wq, L0_attn_a_Wk, L0_attn_a_Wv, L0_attn_a_Wo, L0_attn_b_Wq, L0_attn_b_bq, L0_attn_b_Wk, L0_attn_b_bk, L0_attn_b_Wv, L0_attn_b_bv, L0_attn_b_Wg, L0_attn_b_bg, L0_attn_b_Wo, L0_attn_b_bo, L0_ffn_base_w, L0_ffn_base_b, L0_ffn_gate_w, L0_ffn_lora_A, L0_ffn_lora_B):

    def _L0_attn_a_ref(x, Wq, Wk, Wv, Wo):
        import jax, jax.numpy as jnp
        import numpy as np
        B, N, D = (2, 1024, 128)
        H = 16
        HD = D // H
        EPS = 1e-06

        def _feature_map(a):
            return jax.nn.elu(a) + 1.0
        b, n, d = x.shape
        q = _feature_map((x @ Wq.T).reshape(b, n, H, HD))
        k = _feature_map((x @ Wk.T).reshape(b, n, H, HD))
        v = (x @ Wv.T).reshape(b, n, H, HD)
        kv = jnp.einsum('bnhd,bnhm->bhdm', k, v)
        k_sum = k.sum(axis=1)
        numerator = jnp.einsum('bnhd,bhdm->bnhm', q, kv)
        denominator = jnp.einsum('bnhd,bhd->bnh', q, k_sum)[..., None]
        out = numerator / (denominator + EPS)
        out = out.reshape(b, n, d)
        return out @ Wo.T

    def _L0_attn_b_ref(hidden_states, Wq, bq, Wk, bk, Wv, bv, Wg, bg, Wo, bo):
        import jax, jax.numpy as jnp
        import numpy as np
        import math
        CHUNK = 128
        B, S, H = hidden_states.shape
        D = Wq.shape[1]
        cs = CHUNK
        nC = S // cs
        q = hidden_states @ Wq + bq
        k = hidden_states @ Wk + bk
        v = hidden_states @ Wv + bv
        gate = jax.nn.sigmoid(hidden_states @ Wg + bg)
        qc = q.reshape(B, nC, cs, D)
        kc = k.reshape(B, nC, cs, D)
        vc = v.reshape(B, nC, cs, D)
        gc = gate.reshape(B, nC, cs, D)
        scale = 1.0 / math.sqrt(D)
        attn = jnp.einsum('bncd,bnkd->bnck', qc, kc) * scale
        causal = jnp.tril(jnp.ones((cs, cs), bool))
        attn = jnp.where(causal, attn, -jnp.inf)
        attn = jax.nn.softmax(attn, axis=-1)
        local = jnp.einsum('bnck,bnkd->bncd', attn, vc)

        def step(state, xs):
            qi, ki, vi = xs
            cross = jnp.einsum('bcd,bde->bce', qi, state)
            state = state + jnp.einsum('bcd,bce->bde', ki, vi)
            return (state, cross)
        state0 = jnp.zeros((B, D, D), hidden_states.dtype)
        _, cross = jax.lax.scan(step, state0, (qc.transpose(1, 0, 2, 3), kc.transpose(1, 0, 2, 3), vc.transpose(1, 0, 2, 3)))
        cross = cross.transpose(1, 0, 2, 3)
        out = (local + cross) * gc
        out = out.reshape(B, S, D)
        return out @ Wo + bo

    def _L0_ffn_ref(x, base_w, base_b, gate_w, lora_A, lora_B):
        import jax, jax.numpy as jnp
        import numpy as np
        D_MODEL = 128
        D_OUT = 128
        RANK = 16
        NUM_TRUE = 8
        NUM_NULL = 2
        TOP_K = 2
        SCALING = 32.0 / 16.0
        xf = x.reshape(-1, x.shape[-1])
        logits = jnp.einsum('td,ed->te', xf, gate_w)
        probs = jax.nn.softmax(logits, axis=-1)
        weights, selected = jax.lax.top_k(probs, TOP_K)
        true_mask = (selected < NUM_TRUE).astype(weights.dtype)
        tw = weights * true_mask
        denom = tw.sum(axis=-1, keepdims=True)
        denom = jnp.where(denom > 0, denom, jnp.ones_like(denom))
        nw = tw / denom
        onehot = jax.nn.one_hot(selected, NUM_TRUE, dtype=nw.dtype)
        ew = jnp.einsum('tk,tke->te', nw, onehot)
        z = jnp.einsum('td,erd->ter', xf, lora_A)
        moe = jnp.einsum('ter,te,eor->to', z, ew, lora_B) * SCALING
        base = jnp.einsum('td,od->to', xf, base_w) + base_b
        out = (base + moe).reshape(x.shape[:-1] + (D_OUT,))
        return out
    x = L0_attn_a_x
    x = x + _L0_attn_a_ref(_layernorm(x, axis=-1), L0_attn_a_Wq, L0_attn_a_Wk, L0_attn_a_Wv, L0_attn_a_Wo)
    x = x + _L0_ffn_ref(_layernorm(x, axis=-1), L0_ffn_base_w, L0_ffn_base_b, L0_ffn_gate_w, L0_ffn_lora_A, L0_ffn_lora_B)
    x = x + _L0_attn_b_ref(_layernorm(x, axis=-1), L0_attn_b_Wq, L0_attn_b_bq, L0_attn_b_Wk, L0_attn_b_bk, L0_attn_b_Wv, L0_attn_b_bv, L0_attn_b_Wg, L0_attn_b_bg, L0_attn_b_Wo, L0_attn_b_bo)
    x = x + _L0_ffn_ref(_layernorm(x, axis=-1), L0_ffn_base_w, L0_ffn_base_b, L0_ffn_gate_w, L0_ffn_lora_A, L0_ffn_lora_B)
    return x

_drawn_inputs = setup_inputs


def setup_inputs(seed=0):
    import zlib

    import numpy as np

    out = dict(_drawn_inputs(seed))
    spreads = {'L0_attn_b_bq': (0.0, 0.1),
     'L0_attn_b_bk': (0.0, 0.1),
     'L0_attn_b_bv': (0.0, 0.1),
     'L0_attn_b_bg': (0.0, 0.1),
     'L0_attn_b_bo': (0.0, 0.312)}
    factors = {'L0_attn_a_Wq': 3.365, 'L0_ffn_base_b': 3.31}
    for name, (base, spread) in spreads.items():
        noise = np.random.default_rng([zlib.crc32(name.encode()), seed]).standard_normal(out[name].shape)
        drawn = base * np.exp(spread * noise) if base else spread * noise
        out[name] = jnp.asarray(drawn.astype(out[name].dtype))
    for name, factor in factors.items():
        out[name] = (out[name] * factor).astype(out[name].dtype)
    return out
```

```python
from contextlib import ExitStack

import concourse.bass as bass
from concourse import mybir

F32 = mybir.dt.float32
ALU = mybir.AluOpType
ACT = mybir.ActivationFunctionType
AX = mybir.AxisListType

P = 128
B, S = 2, 1024
TILES = B * S // P
TG = 4
GROUPS = TILES // TG
GB = GROUPS // B
TB = TILES // B
H = 16
HD = P // H
D = 256
EXPERTS, TRUE, RANK = 10, 8, 16
LORA_SCALE = 2.0
PAD = 16
LOWEST = -3.0e38
LN_EPS, DEN_EPS = 1e-5, 1e-6
SHIFT = 0.125
SHIFTS = [0.0, SHIFT, SHIFT, SHIFT]
BIAS_SHARE = 1.0 / (P * SHIFT)
SCORE_SCALE = D ** -0.5
RING = 6

FILLS = [("w_lin", 0), ("w_ffn", 0)]
for g in range(GROUPS):
    FILLS += [("xT0", g), ("q", g), ("k", g)]
    if g % GB == GB - 1:
        FILLS += [("kxT", g // GB), ("kvT", g // GB), ("kvo", g // GB)]
FILLS += [("w_vg", 0), ("w_qk", 0), ("w_m", 0)]
FILLS += [("den", g) for g in range(GROUPS)]
FILLS += [("rden", g) for g in range(GROUPS)]
FILLS += [("lin_out", g) for g in range(GROUPS)]


def ffn_fills(f):
    fills = []
    for g in range(GROUPS):
        fills += [(f"xT{2 * f + 1}", g), (f"logits{f}", g), (f"z{f}", g)]
    fills += [(f"hT{f}", g) for g in range(GROUPS)]
    return fills + [(f"ffn_out{f}", g) for g in range(GROUPS)]


FILLS += ffn_fills(0)
FILLS += [("xT2", g) for g in range(GROUPS)]
for g in range(GROUPS):
    FILLS += [("u", g), ("gram", g)]
for g in range(GROUPS):
    FILLS += [("scores", g), ("gate", 2 * g), ("gate", 2 * g + 1)]
FILLS += [("pT", g) for g in range(GROUPS)]
FILLS += [("wT", g) for g in range(GROUPS)]
for g in range(GROUPS):
    FILLS += [("val", 2 * g), ("val", 2 * g + 1)]
FILLS += [("att_out", g) for g in range(GROUPS)]
FILLS += ffn_fills(1)
KINDS = list(dict.fromkeys(kind for kind, _ in FILLS))
BANK = {fill: n % RING for n, fill in enumerate(FILLS)}
BEFORE = {fill: FILLS[n - RING] for n, fill in enumerate(FILLS) if n >= RING}


def hybrid_block(nc, x, a_wq, a_wk, a_wv, a_wo, b_wq, b_bq, b_wk, b_bk, b_wv, b_bv, b_wg, b_bg, b_wo, b_bo,
                 base_w, base_b, gate_w, lora_a, lora_b, out):
    ctx = ExitStack()
    with ctx:
        def sb(name, shape):
            return ctx.enter_context(nc.sbuf_tensor(name, shape, F32))

        def sem(name):
            return ctx.enter_context(nc.semaphore(name))

        wa_in = sb("wa_in", [P, 4, P])
        wa = sb("wa", [P, 4, P])
        wf_in = sb("wf_in", [P, 4, P])
        wf = sb("wf", [P, 4, P])
        base_col = sb("base_col", [P, 1])
        wf_off = sb("wf_off", [P, 4])
        wb_in = sb("wb_in", [P, 4, D])
        bias_row = sb("bias_row", [1, 4, D])
        share_row = sb("share_row", [1, P])
        w_vg = sb("w_vg", [P, 2, D])
        w_qkT = sb("w_qkT", [P, 4, P])
        w_m = sb("w_m", [P, P])
        w_out = sb("w_out", [P, 2, P])
        bo_all = sb("bo_all", [P, P])
        ident = sb("ident", [P, P])
        centre = sb("centre", [P, P])
        same_head = sb("same_head", [P, P])
        causal = sb("causal", [P, P])
        half_neg = sb("half_neg", [P, TG])

        xs = sb("xs", [P, TILES, P])
        xn = sb("xn", [P, TILES, P + 1])
        xT = sb("xT", [P, TILES, P])
        st = sb("st", [P, 4, TILES, 6])
        mv = sb("mv", [P, 4, TILES, 2])
        rstd = sb("rstd", [P, 4, TILES])
        nshift = sb("nshift", [P, 4, TILES])
        qe = sb("qe", [P, TILES, P])
        ke = sb("ke", [P, TILES, P])
        qT = sb("qT", [P, TILES, P])
        k = sb("k", [P, TILES, P])
        kx = sb("kx", [P, B, P + 1])
        kxT = sb("kxT", [P, B, P])
        kvT = sb("kvT", [P, B, P])
        kvo = sb("kvo", [P, B, P])
        ksum = sb("ksum", [P, B, H])
        rden = sb("rden", [P, TILES, H])
        rden_wide = sb("rden_wide", [P, TILES, P])
        lg = sb("lg", [P, 2, GROUPS, 2, TG, PAD])
        top = sb("top", [P, 2, TILES, 8])
        ex = sb("ex", [P, 2, GROUPS, 2, TG, TRUE])
        ew = sb("ew", [P, 2, TILES, TRUE])
        den = sb("den", [P, 2, TILES])
        hz = qe
        hT = ke
        uT = qT
        gram_in = sb("gram_in", [P, TILES, P])
        gram = sb("gram", [P, TILES, P])
        pr = sb("pr", [P, TILES, P])
        nmax = sb("nmax", [P, TILES])
        rsum = sb("rsum", [P, TILES])
        pT = sb("pT", [P, TILES, P])
        wT = k
        gate = sb("gate", [P, 2, TILES, P])
        gated = sb("gated", [P, 2, TILES, P])

        ps = ctx.enter_context(nc.psum_tensor("ps", [P, RING, 512], F32))
        kx_ps = [ctx.enter_context(nc.psum_tensor(f"kx_ps{b}", [P, 512], F32)) for b in range(B)]

        def bank(kind, n):
            return ps[:, BANK[kind, n], :]

        def tiles_of(kind, n):
            return bank(kind, n).rearrange("p (t c) -> p t c", t=TG)

        filled = {kind: sem(f"filled_{kind}") for kind in KINDS}
        emptied = {kind: sem(f"emptied_{kind}") for kind in KINDS}
        x_in = [sem(f"x_in{g}") for g in range(GROUPS)]
        wa_loaded = sem("wa_loaded")
        wf_loaded = sem("wf_loaded")
        wb_loaded = sem("wb_loaded")
        wo_loaded = sem("wo_loaded")
        consts_step = sem("consts_step")
        pads_set = sem("pads_set")
        wf_centred = sem("wf_centred")
        stats_made = [sem(f"stats_made{n}") for n in range(4)]
        normed = [sem(f"normed{n}") for n in range(4)]
        q_exp = sem("q_exp")
        k_exp = sem("k_exp")
        q_min = sem("q_min")
        k_min = sem("k_min")
        kx_filled = sem("kx_filled")
        kx_copied = sem("kx_copied")
        ksum_made = sem("ksum_made")
        rden_widened = sem("rden_widened")
        exp_args = [sem(f"exp_args{f}") for f in range(2)]
        exps_made = [sem(f"exps_made{f}") for f in range(2)]
        bo_added = sem("bo_added")
        grams_made = sem("grams_made")
        nmax_made = sem("nmax_made")
        probs_exp = sem("probs_exp")
        rsum_made = sem("rsum_made")
        probs_made = sem("probs_made")
        stored = sem("stored")
        dve_step = sem("dve_step")
        pool_step = sem("pool_step")

        x_tok = x.rearrange("b (t p) d -> p (b t) d", p=P)
        out_tok = out.rearrange("b (t p) d -> p (b t) d", p=P)

        def grams_before(i):
            return i // TB * (TB - 1) + i % TB

        def group(g):
            return slice(TG * g, TG * g + TG)

        block = ctx.enter_context(nc.Block())

        @block.sync
        def _(sp):
            for g in range(GROUPS):
                sp.dma_start(xs[:, group(g), :], x_tok[:, group(g), :]).then_inc(x_in[g], 16)
            sp.dma_start(base_col[:, :], base_b.rearrange("(o n) -> o n", n=1)).then_inc(wf_loaded, 16)
            sp.dma_start(wf_in[:, 1, :], base_w).then_inc(wf_loaded, 16)
            sp.dma_start(wf_in[:, 3, :].rearrange("o (e r) -> o e r", r=RANK),
                         lora_b.rearrange("e o r -> o e r")).then_inc(wf_loaded, 16)
            sp.dma_start(wb_in[:, 2, :], b_wv).then_inc(wb_loaded, 16)
            sp.dma_start(wb_in[:, 3, :], b_wg).then_inc(wb_loaded, 16)
            for g in range(GROUPS):
                sp.wait_ge(emptied["ffn_out1"], g + 1)
                sp.dma_start(out_tok[:, group(g), :], xs[:, group(g), :]).then_inc(stored, 16)
            sp.wait_ge(stored, 16 * GROUPS)

        @block.gpsimd
        def _(pool):
            steps = [0]

            def settled(ins):
                steps[0] += 1
                ins.then_inc(pool_step, 1)
                pool.wait_ge(pool_step, steps[0])

            pool.dma_start(w_out[:, :, :], b_wo.rearrange("(h p) o -> p h o", p=P)).then_inc(wo_loaded, 16)
            pool.dma_start(bo_all[:, :], b_bo.partition_broadcast(P)).then_inc(wo_loaded, 16)
            settled(pool.memset(ident[:, :], 0.0))
            pool.affine_select(out=ident[:, :], in_=ident[:, :], compare_op=ALU.not_equal, fill=1.0, base=0,
                               pattern=[[-1, P]], channel_multiplier=1).then_inc(consts_step, 1)
            pool.memset(half_neg[:, :], -0.5)
            pool.memset(xn[:, :, P:P + 1], 1.0)
            pool.memset(same_head[:, :], 1.0)
            settled(pool.memset(causal[:, :], 0.0))

            def normalise(n, g):
                t = group(g)
                pool.wait_ge(stats_made[n], g + 1)
                settled(pool.tensor_scalar(rstd[:, n, t], mv[:, n, t, 1], LN_EPS, None, ALU.add))
                settled(pool.tensor_tensor(rstd[:, n, t], rstd[:, n, t], half_neg[:, :], ALU.pow))
                settled(pool.tensor_tensor(nshift[:, n, t], mv[:, n, t, 0], rstd[:, n, t], ALU.mult))
                settled(pool.tensor_scalar(nshift[:, n, t], nshift[:, n, t], -1.0, SHIFTS[n], ALU.mult, ALU.add))
                for i in range(TG * g, TG * g + TG):
                    last = pool.tensor_scalar(xn[:, i, 0:P], xs[:, i, :], rstd[:, n, i:i + 1], nshift[:, n, i:i + 1],
                                              ALU.mult, ALU.add)
                last.then_inc(normed[n], 1)

            normalise(0, 0)
            pool.memset(share_row[:, :], BIAS_SHARE)
            pool.memset(lg[:, :, :, :, :, :], LOWEST)
            pool.memset(wf_in[:, 2, :], 0.0).then_inc(pads_set, 1)
            pool.tensor_scalar(centre[:, :], ident[:, :], -1.0 / P, None, ALU.add)
            heads = same_head[:, :].rearrange("p (h c) -> p h c", c=HD)
            pool.affine_select(out=causal[:, :], in_=causal[:, :], compare_op=ALU.is_ge, fill=LOWEST, base=0,
                               pattern=[[-1, P]], channel_multiplier=1)
            settled(pool.affine_select(out=heads, in_=heads, compare_op=ALU.is_ge, fill=0.0, base=0,
                                       pattern=[[-HD, H], [0, HD]], channel_multiplier=1))
            pool.affine_select(out=heads, in_=heads, compare_op=ALU.is_ge, fill=0.0, base=HD - 1,
                               pattern=[[HD, H], [0, HD]], channel_multiplier=-1).then_inc(consts_step, 1)
            for g in range(1, GROUPS):
                normalise(0, g)
            for g in range(GROUPS):
                pool.wait_ge(q_exp, g + 1)
                pool.tensor_scalar(qe[:, group(g), :], qe[:, group(g), :], 1.0, None, ALU.min).then_inc(q_min, 1)
                pool.wait_ge(k_exp, g + 1)
                pool.tensor_scalar(ke[:, group(g), :], ke[:, group(g), :], 1.0, None, ALU.min).then_inc(k_min, 1)
            pool.wait_ge(wo_loaded, 32)
            settled(pool.tensor_scalar(w_out[:, :, :], w_out[:, :, :], 0.5, None, ALU.mult))
            for g in range(GROUPS):
                pool.wait_ge(emptied["den"], g + 1)
                pool.tensor_copy(rden_wide[:, group(g), :].rearrange("p t (h c) -> p (t h) c", c=HD),
                                 rden[:, group(g), :].rearrange("p t h -> p (t h)").unsqueeze(2)
                                 .broadcast_to([P, TG * H, HD])).then_inc(rden_widened, 1)
            for g in range(GROUPS):
                normalise(1, g)
            for g in range(GROUPS):
                normalise(2, g)
                pool.wait_ge(normed[2], g + 1)
                pool.tensor_tensor(xs[:, group(g), :], xs[:, group(g), :],
                                   bo_all[:, None, :].broadcast_to([P, TG, P]), ALU.add).then_inc(bo_added, 1)
            for g in range(GROUPS):
                pool.wait_ge(emptied["gram"], g + 1)
                for i in range(TG * g, TG * g + TG):
                    if i % TB == 0:
                        pool.tensor_copy(gram[:, i + 1, :], gram_in[:, i, :]).then_inc(grams_made, 1)
                    elif i % TB < TB - 1:
                        pool.wait_ge(grams_made, grams_before(i))
                        pool.tensor_tensor(gram[:, i + 1, :], gram[:, i, :], gram_in[:, i, :],
                                           ALU.add).then_inc(grams_made, 1)
            for g in range(GROUPS):
                pool.wait_ge(rsum_made, g + 1)
                for i in range(TG * g, TG * g + TG):
                    last = pool.tensor_scalar(pr[:, i, :], pr[:, i, :], rsum[:, i:i + 1], None, ALU.mult)
                last.then_inc(probs_made, 1)
            for g in range(GROUPS):
                normalise(3, g)

        @block.scalar
        def _(act):
            act.dma_start(wa_in[:, 0, :], a_wq).then_inc(wa_loaded, 16)
            act.dma_start(wa_in[:, 1, :], a_wk).then_inc(wa_loaded, 16)
            act.dma_start(wa_in[:, 2, :], a_wv).then_inc(wa_loaded, 16)
            act.dma_start(wa_in[:, 3, :], a_wo).then_inc(wa_loaded, 16)
            act.dma_start(wf_in[:, 0, :], lora_a.rearrange("e r d -> (e r) d")).then_inc(wf_loaded, 16)
            act.wait_ge(pads_set, 1)
            act.dma_start(wf_in[0:EXPERTS, 2, :], gate_w).then_inc(wf_loaded, 16)
            act.dma_start(wb_in[:, 0, :], b_wq).then_inc(wb_loaded, 16)
            act.dma_start(wb_in[:, 1, :], b_wk).then_inc(wb_loaded, 16)
            for n, bias in enumerate((b_bq, b_bk, b_bv, b_bg)):
                act.dma_start(bias_row[:, n, :], bias.rearrange("(a n) -> a n", a=1)).then_inc(wb_loaded, 16)

            def copy_out(kind, n, dst, src=None, scale=1.0):
                act.wait_ge(filled[kind], n + 1)
                act.activation(dst, tiles_of(kind, n) if src is None else src, ACT.Copy,
                               scale=scale).then_inc(emptied[kind], 1)

            copy_out("w_lin", 0, wa[:, :, :])
            copy_out("xT0", 0, xT[:, group(0), :])
            copy_out("w_ffn", 0, wf[:, :, :])

            def setup(b):
                act.wait_ge(kx_filled, b + 1)
                act.activation(kx[:, b, :], kx_ps[b][:, 0:P + 1], ACT.Copy).then_inc(kx_copied, 1)
                copy_out("kxT", b, kxT[:, b, :], bank("kxT", b)[:, 0:P])
                copy_out("kvo", b, kvo[:, b, :], bank("kvo", b)[:, 0:P])

            for g in range(GROUPS):
                if g:
                    copy_out("xT0", g, xT[:, group(g), :])
                act.wait_ge(filled["q"], g + 1)
                act.activation(qe[:, group(g), :], tiles_of("q", g), ACT.Exp).then_inc(q_exp, 1)
                act.wait_ge(filled["k"], g + 1)
                act.activation(ke[:, group(g), :], tiles_of("k", g), ACT.Exp).then_inc(k_exp, 1)
                if g % GB == GB - 1:
                    setup(g // GB)
            copy_out("w_vg", 0, w_vg[:, :, :], bank("w_vg", 0).rearrange("p (a e) -> p a e", a=2))
            copy_out("w_qk", 0, w_qkT[:, :, :])
            copy_out("w_m", 0, w_m[:, :], bank("w_m", 0)[:, 0:P])

            def ffn(f):
                def exps(g):
                    act.wait_ge(exp_args[f], g + 1)
                    act.activation(ex[:, f, g, :, :, :], ex[:, f, g, :, :, :], ACT.Exp).then_inc(exps_made[f], 1)

                for g in range(GROUPS):
                    copy_out(f"xT{2 * f + 1}", g, xT[:, group(g), :])
                    if g:
                        exps(g - 1)
                exps(GROUPS - 1)
                for g in range(GROUPS):
                    copy_out(f"hT{f}", g, hT[:, group(g), :])

            ffn(0)
            for g in range(GROUPS):
                copy_out("xT2", g, xT[:, group(g), :])
            for g in range(GROUPS):
                copy_out("u", g, uT[:, group(g), :])
                copy_out("gram", g, gram_in[:, group(g), :])
            for g in range(GROUPS):
                for a in range(2):
                    act.wait_ge(filled["gate"], 2 * g + a + 1)
                    act.activation(gate[:, a, group(g), :], tiles_of("gate", 2 * g + a), ACT.Tanh,
                                   scale=0.5).then_inc(emptied["gate"], 1)
                act.wait_ge(nmax_made, g + 1)
                for i in range(TG * g, TG * g + TG):
                    last = act.activation(pr[:, i, :], pr[:, i, :], ACT.Exp, bias=nmax[:, i:i + 1],
                                          accum_out=rsum[:, i:i + 1])
                last.then_inc(probs_exp, 1)
            for g in range(GROUPS):
                copy_out("pT", g, pT[:, group(g), :])
            for g in range(GROUPS):
                copy_out("wT", g, wT[:, group(g), :])
            ffn(1)

        @block.vector
        def _(dve):
            steps = [0]

            def settled(ins):
                steps[0] += 1
                ins.then_inc(dve_step, 1)
                dve.wait_ge(dve_step, steps[0])

            def stats(n, g):
                for i in range(TG * g, TG * g + TG):
                    last = dve.bn_stats(st[:, n, i, :], xs[:, i, :])
                settled(last)
                for i in range(TG * g, TG * g + TG):
                    last = dve.bn_aggr(mv[:, n, i, :], st[:, n, i, :])
                last.then_inc(stats_made[n], 1)

            for g in range(GROUPS):
                dve.wait_ge(x_in[g], 16)
                stats(0, g)
            dve.wait_ge(wf_loaded, 16 * 5)
            settled(dve.tensor_reduce(wf_off[:, 0:3], wf_in[:, 0:3, :], AX.X, ALU.add))
            settled(dve.tensor_scalar(wf_off[:, 0:3], wf_off[:, 0:3], -1.0 / P, None, ALU.mult))
            settled(dve.scalar_tensor_tensor(wf_off[:, 1:2], base_col[:, :], BIAS_SHARE, wf_off[:, 1:2],
                                             ALU.mult, ALU.add))
            for n in range(3):
                dve.tensor_scalar(wf_in[:, n, :], wf_in[:, n, :], wf_off[:, n:n + 1], None, ALU.add)
            dve.tensor_scalar(wf_in[:, 3, :], wf_in[:, 3, :], LORA_SCALE, None,
                              ALU.mult).then_inc(wf_centred, 1)

            def setup(b):
                dve.wait_ge(kx_copied, b + 1)
                dve.wait_ge(consts_step, 2)
                dve.tensor_scalar(ksum[:, b, :], same_head[:, 0:P:HD], kx[:, b, P:P + 1], None,
                                  ALU.mult).then_inc(ksum_made, 1)
                dve.wait_ge(filled["kvT"], b + 1)
                dve.tensor_tensor(kvT[:, b, :], bank("kvT", b)[:, 0:P], same_head[:, :],
                                  ALU.mult).then_inc(emptied["kvT"], 1)

            for g in range(GROUPS):
                dve.wait_ge(q_min, g + 1)
                dve.scalar_tensor_tensor(qT[:, group(g), :], tiles_of("q", g), 1.0, qe[:, group(g), :],
                                         ALU.add, ALU.max).then_inc(emptied["q"], 1)
                dve.wait_ge(k_min, g + 1)
                dve.scalar_tensor_tensor(k[:, group(g), :], tiles_of("k", g), 1.0, ke[:, group(g), :],
                                         ALU.add, ALU.max).then_inc(emptied["k"], 1)
                if g % GB == GB - 1:
                    setup(g // GB)
            for g in range(GROUPS):
                dve.wait_ge(filled["den"], g + 1)
                settled(dve.tensor_scalar(rden[:, group(g), :],
                                          bank("den", g)[:, 0:TG * H].rearrange("p (t h) -> p t h", h=H),
                                          DEN_EPS, None, ALU.add))
                dve.reciprocal(rden[:, group(g), :], rden[:, group(g), :]).then_inc(emptied["den"], 1)
            for g in range(GROUPS):
                dve.wait_ge(filled["rden"], g + 1)
                dve.tensor_tensor(qT[:, group(g), :], qT[:, group(g), :], tiles_of("rden", g),
                                  ALU.mult).then_inc(emptied["rden"], 1)

            def residual(kind, g):
                dve.wait_ge(filled[kind], g + 1)
                dve.tensor_tensor(xs[:, group(g), :], xs[:, group(g), :], tiles_of(kind, g),
                                  ALU.add).then_inc(emptied[kind], 1)

            for g in range(GROUPS):
                residual("lin_out", g)
                dve.wait_ge(emptied["lin_out"], g + 1)
                stats(1, g)

            def choose(f, g):
                dve.wait_ge(filled[f"logits{f}"], g + 1)
                if g == 0 and f == 0:
                    dve.wait_ge(pads_set, 1)
                settled_by = dve.tensor_copy(
                    lg[:, f, g, 0, :, 0:EXPERTS],
                    bank(f"logits{f}", g)[:, 0:TG * PAD].rearrange("p (t e) -> p t e", e=PAD)[:, :, 0:EXPERTS])
                settled_by.then_inc(emptied[f"logits{f}"], 1)
                dve.wait_ge(emptied[f"logits{f}"], g + 1)
                for t in range(TG):
                    last = dve.max(top[:, f, TG * g + t, :], lg[:, f, g, 0, t, :])
                settled(last)
                settled(dve.memset(top[:, f, group(g), 2:8], LOWEST))
                for t in range(TG):
                    last = dve.match_replace(lg[:, f, g, 1, t, :], top[:, f, TG * g + t, :], lg[:, f, g, 0, t, :],
                                             LOWEST)
                settled(last)
                dve.tensor_tensor(ex[:, f, g, :, :, :], lg[:, f, g, :, :, 0:TRUE],
                                  top[:, f, group(g), 0:1].unsqueeze(1).broadcast_to([P, 2, TG, TRUE]),
                                  ALU.subtract).then_inc(exp_args[f], 1)

            def weigh(f, g):
                dve.wait_ge(exps_made[f], g + 1)
                t = group(g)
                settled(dve.tensor_tensor(ew[:, f, t, :], ex[:, f, g, 0, :, :], ex[:, f, g, 1, :, :], ALU.subtract))
                settled(dve.tensor_reduce(den[:, f, t], ew[:, f, t, :], AX.X, ALU.add))
                settled(dve.scalar_tensor_tensor(den[:, f, t], den[:, f, t], 0.0, den[:, f, t],
                                                 ALU.is_equal, ALU.add))
                settled(dve.reciprocal(den[:, f, t], den[:, f, t]))
                settled(dve.tensor_tensor(ew[:, f, t, :], ew[:, f, t, :],
                                          den[:, f, t].unsqueeze(2).broadcast_to([P, TG, TRUE]), ALU.mult))
                dve.wait_ge(filled[f"z{f}"], g + 1)
                dve.tensor_tensor(hz[:, t, :].rearrange("p t (e r) -> p (t e) r", r=RANK),
                                  bank(f"z{f}", g).rearrange("p (n r) -> p n r", r=RANK),
                                  ew[:, f, t, :].rearrange("p t e -> p (t e)").unsqueeze(2)
                                  .broadcast_to([P, TG * TRUE, RANK]), ALU.mult).then_inc(emptied[f"z{f}"], 1)

            def ffn(f):
                for g in range(GROUPS):
                    choose(f, g)
                    if g:
                        weigh(f, g - 1)
                weigh(f, GROUPS - 1)
                for g in range(GROUPS):
                    residual(f"ffn_out{f}", g)
                    if f == 0:
                        dve.wait_ge(emptied["ffn_out0"], g + 1)
                        stats(2, g)

            ffn(0)
            for g in range(GROUPS):
                dve.wait_ge(filled["scores"], g + 1)
                dve.scalar_tensor_tensor(pr[:, group(g), :], tiles_of("scores", g), SCORE_SCALE,
                                         causal[:, None, :].broadcast_to([P, TG, P]),
                                         ALU.mult, ALU.add).then_inc(emptied["scores"], 1)
                dve.wait_ge(emptied["scores"], g + 1)
                dve.tensor_reduce(nmax[:, group(g)], pr[:, group(g), :], AX.X, ALU.max,
                                  negate=True).then_inc(nmax_made, 1)
                if g:
                    dve.wait_ge(probs_exp, g)
                    dve.reciprocal(rsum[:, group(g - 1)], rsum[:, group(g - 1)]).then_inc(rsum_made, 1)
            dve.wait_ge(probs_exp, GROUPS)
            dve.reciprocal(rsum[:, group(GROUPS - 1)], rsum[:, group(GROUPS - 1)]).then_inc(rsum_made, 1)
            for g in range(GROUPS):
                for a in range(2):
                    dve.wait_ge(emptied["gate"], 2 * g + a + 1)
                    dve.wait_ge(filled["val"], 2 * g + a + 1)
                    dve.scalar_tensor_tensor(gated[:, a, group(g), :], gate[:, a, group(g), :], 1.0,
                                             tiles_of("val", 2 * g + a), ALU.add,
                                             ALU.mult).then_inc(emptied["val"], 1)
            for g in range(GROUPS):
                dve.wait_ge(bo_added, g + 1)
                residual("att_out", g)
                dve.wait_ge(emptied["att_out"], g + 1)
                stats(3, g)
            ffn(1)

        @block.tensor
        def _(pe):
            def take(kind, n):
                if (kind, n) in BEFORE:
                    before, m = BEFORE[kind, n]
                    pe.wait_ge(emptied[before], m + 1)
                return bank(kind, n)

            def transposes(kind, g, src):
                dst = take(kind, g)
                for t in range(TG):
                    last = pe.transpose(dst[:, P * t:P * t + P], src(TG * g + t), ident[:, :])
                last.then_inc(filled[kind], 1)

            def normed_rows(n, g):
                pe.wait_ge(normed[n], g + 1)
                transposes(f"xT{n}", g, lambda i: xn[:, i, 0:P])

            def wide(kind, n, lhs, rhs):
                pe.matmul(take(kind, n), lhs, rhs, start=True, stop=True).then_inc(filled[kind], 1)

            def by_tile(kind, n, lhs, rhs, width=P, pitch=P):
                dst = take(kind, n)
                for t in range(TG):
                    last = pe.matmul(dst[:, pitch * t:pitch * t + width], lhs(TG * n + t), rhs(TG * n + t),
                                     start=True, stop=True)
                last.then_inc(filled[kind], 1)

            pe.wait_ge(consts_step, 1)
            pe.wait_ge(wa_loaded, 64)
            transposes("w_lin", 0, lambda n: wa_in[:, n, :])
            pe.wait_ge(wf_centred, 1)
            transposes("w_ffn", 0, lambda n: wf_in[:, n, :])

            def setup(b):
                pe.wait_ge(kx_copied, b + 1)
                pe.transpose(take("kxT", b)[:, 0:P], kx[:, b, 0:P], ident[:, :]).then_inc(filled["kxT"], 1)
                pe.wait_ge(emptied["kxT"], b + 1)
                pe.matmul(take("kvT", b)[:, 0:P], wa[:, 2, :], kxT[:, b, :], start=True,
                          stop=True).then_inc(filled["kvT"], 1)
                pe.wait_ge(emptied["kvT"], b + 1)
                pe.matmul(take("kvo", b)[:, 0:P], kvT[:, b, :], wa[:, 3, :], start=True,
                          stop=True).then_inc(filled["kvo"], 1)

            pe.wait_ge(emptied["w_lin"], 1)
            for g in range(GROUPS):
                normed_rows(0, g)
                pe.wait_ge(emptied["xT0"], g + 1)
                wide("q", g, wa[:, 0, :], xT[:, group(g), :])
                by_tile("k", g, lambda i: xT[:, i, :], lambda i: wa[:, 1, :])
                pe.wait_ge(emptied["k"], g + 1)
                for i in range(TG * g, TG * g + TG):
                    last = pe.matmul(kx_ps[i // TB][:, 0:P + 1], k[:, i, :], xn[:, i, :], start=i % TB == 0,
                                     stop=i % TB == TB - 1)
                if g % GB == GB - 1:
                    last.then_inc(kx_filled, 1)
                    setup(g // GB)

            pe.wait_ge(wb_loaded, 16 * 8)
            pe.wait_ge(consts_step, 2)
            dst = take("w_vg", 0)
            pe.matmul(dst, centre[:, :], wb_in[:, 2:4, :], start=True, stop=False)
            pe.matmul(dst, share_row[:, :], bias_row[:, 2:4, :], start=False, stop=True).then_inc(filled["w_vg"], 1)
            dst = take("w_qk", 0)
            for n in range(4):
                cols, half = dst[:, P * n:P * n + P], slice(P * (n % 2), P * (n % 2) + P)
                pe.matmul(cols, wb_in[:, n // 2, half], centre[:, :], start=True, stop=False)
                last = pe.matmul(cols, bias_row[:, n // 2, half], share_row[:, :], start=False, stop=True)
            last.then_inc(filled["w_qk"], 1)
            pe.wait_ge(emptied["w_qk"], 1)
            dst = take("w_m", 0)[:, 0:P]
            pe.matmul(dst, w_qkT[:, 0, :], w_qkT[:, 2, :], start=True, stop=False)
            pe.matmul(dst, w_qkT[:, 1, :], w_qkT[:, 3, :], start=False, stop=True).then_inc(filled["w_m"], 1)

            for g in range(GROUPS):
                pe.wait_ge(ksum_made, g // GB + 1)
                by_tile("den", g, lambda i: qT[:, i, :], lambda i: ksum[:, i // TB, :], width=H, pitch=H)
            for g in range(GROUPS):
                pe.wait_ge(rden_widened, g + 1)
                transposes("rden", g, lambda i: rden_wide[:, i, :])
            for g in range(GROUPS):
                pe.wait_ge(emptied["kvo"], g // GB + 1)
                pe.wait_ge(emptied["rden"], g + 1)
                by_tile("lin_out", g, lambda i: qT[:, i, :], lambda i: kvo[:, i // TB, :])

            def ffn(f):
                for g in range(GROUPS):
                    normed_rows(2 * f + 1, g)
                    if g == 0:
                        pe.wait_ge(emptied["w_ffn"], 1)
                    pe.wait_ge(emptied[f"xT{2 * f + 1}"], g + 1)
                    by_tile(f"logits{f}", g, lambda i: xT[:, i, :], lambda i: wf[:, 2, 0:EXPERTS], EXPERTS, PAD)
                    by_tile(f"z{f}", g, lambda i: xT[:, i, :], lambda i: wf[:, 0, :])
                for g in range(GROUPS):
                    pe.wait_ge(emptied[f"z{f}"], g + 1)
                    transposes(f"hT{f}", g, lambda i: hz[:, i, :])
                for g in range(GROUPS):
                    pe.wait_ge(emptied[f"hT{f}"], g + 1)
                    dst = take(f"ffn_out{f}", g)
                    for t in range(TG):
                        i, cols = TG * g + t, dst[:, P * t:P * t + P]
                        pe.matmul(cols, xT[:, i, :], wf[:, 1, :], start=True, stop=False)
                        last = pe.matmul(cols, hT[:, i, :], wf[:, 3, :], start=False, stop=True)
                    last.then_inc(filled[f"ffn_out{f}"], 1)

            ffn(0)
            for g in range(GROUPS):
                normed_rows(2, g)
            pe.wait_ge(emptied["w_m"], 1)
            for g in range(GROUPS):
                pe.wait_ge(emptied["xT2"], g + 1)
                wide("u", g, w_m[:, :], xT[:, group(g), :])
                by_tile("gram", g, lambda i: xn[:, i, 0:P], lambda i: xn[:, i, 0:P])
            for g in range(GROUPS):
                pe.wait_ge(emptied["u"], g + 1)
                by_tile("scores", g, lambda i: uT[:, i, :], lambda i: xT[:, i, :])
                for a in range(2):
                    wide("gate", 2 * g + a, w_vg[:, 1, P * a:P * a + P], xT[:, group(g), :])
            for g in range(GROUPS):
                pe.wait_ge(probs_made, g + 1)
                transposes("pT", g, lambda i: pr[:, i, :])
            for g in range(GROUPS):
                pe.wait_ge(emptied["pT"], g + 1)
                dst = take("wT", g)
                for t in range(TG):
                    i, cols = TG * g + t, dst[:, P * t:P * t + P]
                    last = pe.matmul(cols, xn[:, i, 0:P], pT[:, i, :], start=True, stop=i % TB == 0)
                    if i % TB:
                        pe.wait_ge(grams_made, grams_before(i))
                        last = pe.matmul(cols, gram[:, i, :], uT[:, i, :], start=False, stop=True)
                last.then_inc(filled["wT"], 1)
            for g in range(GROUPS):
                pe.wait_ge(emptied["wT"], g + 1)
                for a in range(2):
                    wide("val", 2 * g + a, w_vg[:, 0, P * a:P * a + P], wT[:, group(g), :])
            for g in range(GROUPS):
                pe.wait_ge(emptied["val"], 2 * g + 2)
                dst = take("att_out", g)
                for t in range(TG):
                    i, cols = TG * g + t, dst[:, P * t:P * t + P]
                    pe.matmul(cols, gated[:, 0, i, :], w_out[:, 0, :], start=True, stop=False)
                    last = pe.matmul(cols, gated[:, 1, i, :], w_out[:, 1, :], start=False, stop=True)
                last.then_inc(filled["att_out"], 1)
            ffn(1)


_INS = ["L0_attn_a_x", "L0_attn_a_Wq", "L0_attn_a_Wk", "L0_attn_a_Wv", "L0_attn_a_Wo",
        "L0_attn_b_Wq", "L0_attn_b_bq", "L0_attn_b_Wk", "L0_attn_b_bk", "L0_attn_b_Wv", "L0_attn_b_bv",
        "L0_attn_b_Wg", "L0_attn_b_bg", "L0_attn_b_Wo", "L0_attn_b_bo",
        "L0_ffn_base_w", "L0_ffn_base_b", "L0_ffn_gate_w", "L0_ffn_lora_A", "L0_ffn_lora_B"]


def kernel(**inputs):
    import numpy as np
    import concourse.bacc as bacc
    from concourse.bass_utils import run_bass_kernel_spmd

    nc = bacc.Bacc("TRN2", target_bir_lowering=False, num_devices=1)
    arrays, args = {}, []
    for name in _INS:
        a = np.ascontiguousarray(inputs[name])
        arrays[f"in_{name}"] = a
        args.append(nc.dram_tensor(f"in_{name}", a.shape, mybir.dt.from_np(a.dtype), kind="ExternalInput").ap())
    out = nc.dram_tensor("out", [B, S, P], F32, kind="ExternalOutput").ap()
    hybrid_block(nc, *args, out)
    return run_bass_kernel_spmd(nc, [arrays], core_ids=[0]).results[0]["out"]
```

```python
from contextlib import ExitStack

import concourse.bass as bass
from concourse import mybir

F32 = mybir.dt.float32
ALU = mybir.AluOpType
ACT = mybir.ActivationFunctionType
AX = mybir.AxisListType

P = 128
B, S = 2, 1024
TILES = B * S // P
TG = 4
GROUPS = TILES // TG
GB = GROUPS // B
TB = TILES // B
H = 16
HD = P // H
D = 256
EXPERTS, TRUE, RANK = 10, 8, 16
LORA_SCALE = 2.0
PAD = 16
LOWEST, TINY = -1.0e30, 1.2e-38
LN_EPS, DEN_EPS = 1e-5, 1e-6
SHIFT = 0.125
BIAS_SHARE = 1.0 / (P * SHIFT)
SCORE_SCALE = D ** -0.5
BANKS = 8

PLACES = [("stats0", 0), ("norm0", 1), ("xT0", 2), ("qk", 3), ("feature", 4), ("kx", 5),
          ("den", 11), ("widen", 12), ("rden", 13), ("lin_out", 14),
          ("xT1", 16), ("z0", 18), ("exps0", 19), ("weigh0", 20), ("hT0", 21), ("ffn_out0", 22),
          ("norm2", 24), ("xT2", 25), ("u", 26), ("scores", 27), ("gate", 28), ("softmax", 28.5), ("probs", 29.5),
          ("pT", 30.5), ("wT", 31.5), ("val", 32.5), ("att_out", 34),
          ("xT3", 36), ("z1", 38), ("exps1", 39), ("weigh1", 40), ("hT1", 41), ("ffn_out1", 42)]
STARTS = [0, 0.1, 4, 4.1]
ROW_PLACES = [("kxT", 6), ("kvT", 7), ("kvo", 8)]
WEIGHT_PLACES = [("w_lin", 0.5), ("w_ffn", 5.5), ("w_b", 9)]
ORDER = sorted([(place + STARTS[g], stage, g) for stage, place in PLACES for g in range(GROUPS)]
               + [(place + STARTS[GB * b + GB - 1], stage, b) for stage, place in ROW_PLACES for b in range(B)]
               + [(place, stage, 0) for stage, place in WEIGHT_PLACES])
ORDER = [(item.split(":")[0], int(item.split(":")[1])) for item in """
w_lin:0 stats0:0 stats0:1 norm0:0 norm0:1 stats0:2 norm0:2 xT0:0 xT0:1 xT0:2 qk:0 feature:0 qk:1 feature:1
stats0:3 w_b:0 kx:0 norm0:3 kx:1 xT0:3 w_ffn:0 qk:2 kxT:0 feature:2 qk:3 den:0 kvT:0 den:1 widen:0
feature:3 widen:1 kx:2 kvo:0 rden:0 rden:1 lin_out:0 kx:3 xT1:0 kxT:1 z0:0 den:2 exps0:0 lin_out:1 widen:2
rden:2 kvT:1 weigh0:0 xT1:1 z0:1 den:3 kvo:1 widen:3 hT0:0 exps0:1 lin_out:2 weigh0:1 ffn_out0:0 rden:3
xT1:2 hT0:1 z0:2 exps0:2 norm2:0 weigh0:2 lin_out:3 ffn_out0:1 xT1:3 xT2:0 hT0:2 z0:3 u:0 norm2:1 scores:0
ffn_out0:2 softmax:0 probs:0 gate:0 xT2:1 exps0:3 weigh0:3 gate:1 u:1 hT0:3 pT:0 norm2:2 scores:1
ffn_out0:3 xT2:2 softmax:1 wT:0 u:2 norm2:3 probs:1 val:0 pT:1 xT2:3 scores:2 att_out:0 wT:1 u:3 softmax:2
xT3:0 probs:2 val:1 scores:3 z1:0 pT:2 gate:2 att_out:1 softmax:3 probs:3 exps1:0 wT:2 gate:3 weigh1:0
xT3:1 pT:3 val:2 z1:1 att_out:2 exps1:1 weigh1:1 wT:3 xT3:2 val:3 z1:2 att_out:3 hT1:0 exps1:2 weigh1:2
hT1:1 xT3:3 z1:3 ffn_out1:0 exps1:3 hT1:2 weigh1:3 ffn_out1:1 ffn_out1:2 hT1:3 ffn_out1:3
""".split()]

STAGE_FILLS = {"qk": ["q", "k"], "u": ["u", "gram"], "w_b": ["w_vg", "w_qk", "w_m"]}
NO_FILLS = {"feature", "widen", "weigh0", "weigh1", "exps0", "exps1", "softmax", "probs"}
READ_IN = {"z0": "weigh0", "z1": "weigh1"}
WHEN = {item: at for at, item in enumerate(ORDER)}
FILLS = []
for (stage, n), at in WHEN.items():
    if stage in ("gate", "val"):
        FILLS += [(stage, 2 * n, at, at), (stage, 2 * n + 1, at, at)]
    elif stage == "kx":
        if n % GB == 0:
            FILLS += [(stage, n // GB, at, WHEN[stage, n + GB - 1])]
    elif stage not in NO_FILLS and not stage.startswith(("stats", "norm")):
        FILLS += [(kind, n, at, WHEN[READ_IN.get(stage, stage), n]) for kind in STAGE_FILLS.get(stage, [stage])]
KINDS = list(dict.fromkeys(fill[0] for fill in FILLS))
BANK, BEFORE = {}, {}
holder = {}
done = [-BANKS + i for i in range(BANKS)]
for kind, n, at, last in FILLS:
    width = 2 if kind in ("z0", "z1") else 1
    first = min(range(BANKS + 1 - width), key=lambda i: (max(done[i:i + width]), i))
    BANK[kind, n] = first
    BEFORE[kind, n] = list(dict.fromkeys(holder[i] for i in range(first, first + width) if i in holder))
    for i in range(first, first + width):
        holder[i], done[i] = (kind, n), last + len(BANK) / len(FILLS)


def hybrid_block(nc, x, a_wq, a_wk, a_wv, a_wo, b_wq, b_bq, b_wk, b_bk, b_wv, b_bv, b_wg, b_bg, b_wo, b_bo,
                 base_w, base_b, gate_w, lora_a, lora_b, out):
    ctx = ExitStack()
    with ctx:
        def sb(name, shape):
            return ctx.enter_context(nc.sbuf_tensor(name, shape, F32))

        def sem(name):
            return ctx.enter_context(nc.semaphore(name))

        wa_in = sb("wa_in", [P, 4, P])
        wa = sb("wa", [P, 4, P])
        wf_in = sb("wf_in", [P, 4, P])
        wf = sb("wf", [P, 4, P])
        base_all = sb("base_all", [P, P])
        off = sb("off", [P, 2, 3])
        wb_in = sb("wb_in", [P, 4, D])
        bias_row = sb("bias_row", [1, 4, D])
        share_row = sb("share_row", [1, P])
        w_vg = sb("w_vg", [P, 2, D])
        w_qkT = sb("w_qkT", [P, 4, P])
        w_m = sb("w_m", [P, P])
        w_out = sb("w_out", [P, 2, P])
        bo_all = sb("bo_all", [P, P])
        ident = sb("ident", [P, P])
        centre = sb("centre", [P, P])
        same_head = sb("same_head", [P, P])
        causal = sb("causal", [P, P])
        half_neg = sb("half_neg", [P, TG])
        warm = sb("warm", [P, 1])

        xs = sb("xs", [P, TILES, P])
        xs_bias = sb("xs_bias", [P, TILES, P])
        xn = sb("xn", [P, TILES, P + 1])
        xT = sb("xT", [P, TILES, P])
        st = sb("st", [P, 4, TILES, 6])
        mv = sb("mv", [P, 4, TILES, 2])
        rstd = sb("rstd", [P, 4, TILES])
        nshift = sb("nshift", [P, TILES])
        qe = sb("qe", [P, TILES, P])
        ke = sb("ke", [P, TILES, P])
        qT = sb("qT", [P, TILES, P])
        k = sb("k", [P, TILES, P])
        kx = sb("kx", [P, B, P + 1])
        kxT = sb("kxT", [P, B, P])
        kvT = sb("kvT", [P, B, P])
        kvo = sb("kvo", [P, B, P])
        ksum = sb("ksum", [P, B, H])
        rden = sb("rden", [P, TILES, H])
        rden_wide = sb("rden_wide", [P, TILES, P])
        lg = sb("lg", [P, 2, GROUPS, 2, TG, PAD])
        top = sb("top", [P, 2, TILES, 8])
        ex = sb("ex", [P, 2, GROUPS, 2, TG, TRUE])
        picked = sb("picked", [P, 2, TILES, TRUE + 1])
        ew = sb("ew", [P, 2, TILES, TRUE])
        den = sb("den", [P, 2, TILES])
        hz = qe
        hT = ke
        uT = qT
        gram_in = sb("gram_in", [P, TILES, P])
        gram = sb("gram", [P, TILES, P])
        pr = sb("pr", [P, TILES, P])
        nmax = sb("nmax", [P, TILES])
        rsum = sb("rsum", [P, TILES])
        pT = sb("pT", [P, TILES, P])
        wT = k
        gate = sb("gate", [P, 2, TILES, P])
        gated = sb("gated", [P, 2, TILES, P])

        ps = ctx.enter_context(nc.psum_tensor("ps", [P, BANKS, 512], F32))

        def bank(kind, n):
            return ps[:, BANK[kind, n], :]

        def tiles_of(kind, n):
            return bank(kind, n).rearrange("p (t c) -> p t c", t=TG)

        def z_and_logits(f, n):
            first = BANK[f"z{f}", n]
            return ps[:, first:first + 2, :].rearrange("p a c -> p (a c)").rearrange("p (t c) -> p t c", t=TG)

        filled = {kind: sem(f"filled_{kind}") for kind in KINDS}
        emptied = {kind: sem(f"emptied_{kind}") for kind in KINDS}
        x_in = [sem(f"x_in{g}") for g in range(GROUPS)]
        wa_loaded = sem("wa_loaded")
        wf_loaded = sem("wf_loaded")
        wb_loaded = sem("wb_loaded")
        wo_loaded = sem("wo_loaded")
        consts_step = sem("consts_step")
        pads_set = sem("pads_set")
        wf_centred = sem("wf_centred")
        stats_made = [sem(f"stats_made{n}") for n in range(4)]
        normed = [sem(f"normed{n}") for n in range(4)]
        rstd_made = [sem(f"rstd_made{n}") for n in range(4)]
        gate_w_loaded = sem("gate_w_loaded")
        q_made = sem("q_made")
        k_made = sem("k_made")
        ksum_made = sem("ksum_made")
        rden_widened = sem("rden_widened")
        logits_copied = [sem(f"logits_copied{f}") for f in range(2)]
        exp_args = [sem(f"exp_args{f}") for f in range(2)]
        exps_made = [sem(f"exps_made{f}") for f in range(2)]
        bias_added = [sem(f"bias_added{n}") for n in range(4)]
        wa_centred = sem("wa_centred")
        grams_made = sem("grams_made")
        nshift_made = sem("nshift_made")
        nmax_made = sem("nmax_made")
        probs_exp = sem("probs_exp")
        rsum_made = sem("rsum_made")
        probs_made = sem("probs_made")
        stored = sem("stored")
        dve_step = sem("dve_step")
        tile_stats = sem("tile_stats")
        pool_step = sem("pool_step")

        x_tok = x.rearrange("b (t p) d -> p (b t) d", p=P)
        out_tok = out.rearrange("b (t p) d -> p (b t) d", p=P)

        def grams_before(i):
            return i // TB * (TB - 1) + i % TB

        def group(g):
            return slice(TG * g, TG * g + TG)

        block = ctx.enter_context(nc.Block())

        @block.sync
        def _(sp):
            def load_x(g):
                sp.dma_start(xs[:, group(g), :], x_tok[:, group(g), :]).then_inc(x_in[g], 16)

            load_x(0)
            sp.dma_start(wa_in[:, 0, :], a_wq).then_inc(wa_loaded, 16)
            sp.dma_start(wa_in[:, 1, :], a_wk).then_inc(wa_loaded, 16)
            for g in range(1, GROUPS):
                load_x(g)
            sp.dma_start(wf_in[:, 0, :], lora_a.rearrange("e r d -> (e r) d")).then_inc(wf_loaded, 16)
            sp.dma_start(wf_in[:, 2, :], base_w).then_inc(wf_loaded, 16)
            sp.dma_start(wf_in[:, 3, :].rearrange("o (e r) -> o e r", r=RANK),
                         lora_b.rearrange("e o r -> o e r")).then_inc(wf_loaded, 16)
            for n, w in enumerate((b_wq, b_wk, b_wv, b_wg)):
                sp.dma_start(wb_in[:, n, :], w).then_inc(wb_loaded, 16)
            for n, bias in enumerate((b_bq, b_bk, b_bv, b_bg)):
                sp.dma_start(bias_row[:, n, :], bias.rearrange("(a n) -> a n", a=1)).then_inc(wb_loaded, 16)
            for g in range(GROUPS):
                sp.wait_ge(emptied["ffn_out1"], g + 1)
                sp.dma_start(out_tok[:, group(g), :], xs[:, group(g), :]).then_inc(stored, 16)
            sp.wait_ge(stored, 16 * GROUPS)

        @block.gpsimd
        def _(pool):
            steps = [0]

            def settled(ins):
                steps[0] += 1
                ins.then_inc(pool_step, 1)
                pool.wait_ge(pool_step, steps[0])

            settled(pool.memset(ident[:, :], 0.0))
            pool.affine_select(out=ident[:, :], in_=ident[:, :], compare_op=ALU.not_equal, fill=1.0, base=0,
                               pattern=[[-1, P]], channel_multiplier=1).then_inc(consts_step, 1)
            pool.memset(half_neg[:, :], -0.5)
            settled(pool.memset(wf_in[:, 1, :], 0.0))
            pool.dma_start(wf_in[0:EXPERTS, 1, :], gate_w).then_inc(gate_w_loaded, 16)
            pool.memset(xn[:, :, P:P + 1], 1.0)
            pool.memset(same_head[:, :], 1.0)
            settled(pool.memset(causal[:, :], 0.0))

            def inverse_deviation(n, g):
                t = group(g)
                pool.wait_ge(stats_made[n], g + 1)
                settled(pool.tensor_scalar(rstd[:, n, t], mv[:, n, t, 1], LN_EPS, None, ALU.add))
                pool.tensor_tensor(rstd[:, n, t], rstd[:, n, t], half_neg[:, :], ALU.pow).then_inc(rstd_made[n], 1)

            def constants():
                pool.memset(share_row[:, :], BIAS_SHARE)
                pool.memset(picked[:, :, :, TRUE:TRUE + 1], TINY)
                pool.memset(lg[:, :, :, :, :, :], LOWEST).then_inc(pads_set, 1)
                pool.tensor_scalar(centre[:, :], ident[:, :], -1.0 / P, None, ALU.add)
                heads = same_head[:, :].rearrange("p (h c) -> p h c", c=HD)
                pool.affine_select(out=causal[:, :], in_=causal[:, :], compare_op=ALU.is_ge, fill=LOWEST, base=0,
                                   pattern=[[-1, P]], channel_multiplier=1)
                settled(pool.affine_select(out=heads, in_=heads, compare_op=ALU.is_ge, fill=0.0, base=0,
                                           pattern=[[-HD, H], [0, HD]], channel_multiplier=1))
                pool.affine_select(out=heads, in_=heads, compare_op=ALU.is_ge, fill=0.0, base=HD - 1,
                                   pattern=[[HD, H], [0, HD]], channel_multiplier=-1).then_inc(consts_step, 1)
                pool.dma_start(w_out[:, :, :], b_wo.rearrange("(h p) o -> p h o", p=P)).then_inc(wo_loaded, 16)
                pool.dma_start(bo_all[:, :], b_bo.partition_broadcast(P)).then_inc(wo_loaded, 16)
                pool.dma_start(base_all[:, :], base_b.partition_broadcast(P)).then_inc(wo_loaded, 16)

            def add_bias(n, g, bias):
                pool.tensor_tensor(xs_bias[:, group(g), :], xs[:, group(g), :],
                                   bias[:, None, :].broadcast_to([P, TG, P]), ALU.add).then_inc(bias_added[n], 1)

            def sum_grams(g):
                pool.wait_ge(emptied["gram"], g + 1)
                for i in range(TG * g, TG * g + TG):
                    if i % TB == 0:
                        pool.tensor_copy(gram[:, i + 1, :], gram_in[:, i, :]).then_inc(grams_made, 1)
                    elif i % TB < TB - 1:
                        pool.wait_ge(grams_made, grams_before(i))
                        pool.tensor_tensor(gram[:, i + 1, :], gram[:, i, :], gram_in[:, i, :],
                                           ALU.add).then_inc(grams_made, 1)

            for stage, n in ORDER:
                if stage == "stats0":
                    inverse_deviation(0, n)
                elif stage == "w_lin":
                    constants()
                elif stage == "w_b":
                    pool.wait_ge(wo_loaded, 48)
                    settled(pool.tensor_scalar(w_out[:, :, :], w_out[:, :, :], 0.5, None, ALU.mult))
                elif stage == "lin_out":
                    inverse_deviation(1, n)
                    add_bias(1, n, base_all)
                elif stage == "ffn_out0":
                    inverse_deviation(2, n)
                    add_bias(2, n, bo_all)
                elif stage == "u":
                    sum_grams(n)
                elif stage == "att_out":
                    inverse_deviation(3, n)
                    add_bias(3, n, base_all)

        @block.scalar
        def _(act):
            act.dma_start(wa_in[:, 2, :], a_wv).then_inc(wa_loaded, 16)
            act.dma_start(wa_in[:, 3, :], a_wo).then_inc(wa_loaded, 16)
            act.wait_ge(consts_step, 1)
            act.activation(warm[:, :], ident[:, 0:1], ACT.Exp)

            def copy_out(kind, n, dst, src=None):
                act.wait_ge(filled[kind], n + 1)
                act.activation(dst, tiles_of(kind, n) if src is None else src, ACT.Copy).then_inc(emptied[kind], 1)

            def feature_parts(kind, g, positive, exponential):
                act.wait_ge(filled[kind], g + 1)
                act.activation(positive[:, group(g), :], tiles_of(kind, g), ACT.Relu)
                act.activation(exponential[:, group(g), :], tiles_of(kind, g), ACT.Exp).then_inc(emptied[kind], 1)

            for stage, n in ORDER:
                if stage == "norm0":
                    act.wait_ge(rstd_made[0], n + 1)
                    for i in range(TG * n, TG * n + TG):
                        last = act.activation(xn[:, i, 0:P], xs[:, i, :], ACT.Copy, scale=rstd[:, 0, i:i + 1])
                    last.then_inc(normed[0], 1)
                elif stage == "norm2":
                    act.wait_ge(nshift_made, n + 1)
                    for i in range(TG * n, TG * n + TG):
                        last = act.activation(xn[:, i, 0:P], xs[:, i, :], ACT.Identity, bias=nshift[:, i:i + 1],
                                              scale=rstd[:, 2, i:i + 1])
                    last.then_inc(normed[2], 1)
                elif stage == "w_lin":
                    copy_out("w_lin", 0, wa[:, :, :])
                elif stage == "w_ffn":
                    copy_out("w_ffn", 0, wf[:, :, :])
                elif stage == "w_b":
                    copy_out("w_vg", 0, w_vg[:, :, :], bank("w_vg", 0).rearrange("p (a e) -> p a e", a=2))
                    copy_out("w_qk", 0, w_qkT[:, :, :])
                    copy_out("w_m", 0, w_m[:, :], bank("w_m", 0)[:, 0:P])
                elif stage in ("xT0", "xT1", "xT2", "xT3"):
                    copy_out(stage, n, xT[:, group(n), :])
                elif stage == "qk":
                    feature_parts("q", n, qT, qe)
                    feature_parts("k", n, k, ke)
                elif stage == "kx":
                    if n % GB == GB - 1:
                        b = n // GB
                        copy_out("kx", b, kx[:, b, :], bank("kx", b)[:, 0:P + 1])
                elif stage == "kxT":
                    copy_out("kxT", n, kxT[:, n, :], bank("kxT", n)[:, 0:P])
                elif stage == "kvo":
                    copy_out("kvo", n, kvo[:, n, :], bank("kvo", n)[:, 0:P])
                elif stage == "widen":
                    act.wait_ge(emptied["den"], n + 1)
                    act.activation(rden_wide[:, group(n), :].rearrange("p t (h c) -> p (t h) c", c=HD),
                                   rden[:, group(n), :].rearrange("p t h -> p (t h)").unsqueeze(2)
                                   .broadcast_to([P, TG * H, HD]), ACT.Copy).then_inc(rden_widened, 1)
                elif stage in ("z0", "z1"):
                    f = int(stage[1])
                    if f == 0:
                        act.wait_ge(pads_set, 1)
                    act.wait_ge(filled[stage], n + 1)
                    act.activation(lg[:, f, n, 0, :, 0:EXPERTS], z_and_logits(f, n)[:, :, P:P + EXPERTS],
                                   ACT.Copy).then_inc(logits_copied[f], 1)
                elif stage in ("exps0", "exps1"):
                    f = int(stage[4])
                    act.wait_ge(exp_args[f], n + 1)
                    act.activation(ex[:, f, n, :, :, :], ex[:, f, n, :, :, :], ACT.Exp).then_inc(exps_made[f], 1)
                elif stage in ("hT0", "hT1"):
                    copy_out(stage, n, hT[:, group(n), :])
                elif stage == "u":
                    copy_out("u", n, uT[:, group(n), :])
                    copy_out("gram", n, gram_in[:, group(n), :])
                elif stage == "gate":
                    for a in range(2):
                        act.wait_ge(filled["gate"], 2 * n + a + 1)
                        act.activation(gate[:, a, group(n), :], tiles_of("gate", 2 * n + a), ACT.Tanh,
                                       scale=0.5).then_inc(emptied["gate"], 1)
                elif stage == "softmax":
                    act.wait_ge(nmax_made, n + 1)
                    for i in range(TG * n, TG * n + TG):
                        last = act.activation(pr[:, i, :], pr[:, i, :], ACT.Exp, bias=nmax[:, i:i + 1],
                                              accum_out=rsum[:, i:i + 1])
                    last.then_inc(probs_exp, 1)
                elif stage == "pT":
                    copy_out("pT", n, pT[:, group(n), :])
                elif stage == "wT":
                    copy_out("wT", n, wT[:, group(n), :])

        @block.vector
        def _(dve):
            steps = [0]
            counted = [0]

            def settled(ins):
                steps[0] += 1
                ins.then_inc(dve_step, 1)
                dve.wait_ge(dve_step, steps[0])

            def stats(n, g):
                for i in range(TG * g, TG * g + TG):
                    dve.bn_stats(st[:, n, i, :], xs[:, i, :]).then_inc(tile_stats, 1)
                    counted[0] += 1
                for t in range(TG):
                    i = TG * g + t
                    dve.wait_ge(tile_stats, counted[0] - TG + t + 1)
                    last = dve.bn_aggr(mv[:, n, i, :], st[:, n, i, :])
                last.then_inc(stats_made[n], 1)

            def centre_rows(n, rows, made):
                settled(dve.tensor_reduce(off[:, n, :], rows, AX.X, ALU.add))
                settled(dve.tensor_scalar(off[:, n, :], off[:, n, :], -1.0 / P, None, ALU.mult))
                dve.tensor_tensor(rows, rows, off[:, n, :].unsqueeze(2).broadcast_to([P, 3, P]),
                                  ALU.add).then_inc(made, 1)

            def feature(kind, g, positive, exponential, made):
                dve.wait_ge(emptied[kind], g + 1)
                dve.scalar_tensor_tensor(positive[:, group(g), :], exponential[:, group(g), :], 1.0,
                                         positive[:, group(g), :], ALU.min, ALU.add).then_inc(made, 1)

            def residual_scaled(n, kind, g):
                dve.wait_ge(filled[kind], g + 1)
                dve.wait_ge(bias_added[n], g + 1)
                for t in range(TG):
                    i = TG * g + t
                    last = dve.scalar_tensor_tensor(xs[:, i, :], tiles_of(kind, g)[:, t, :], rstd[:, n, i:i + 1],
                                                    xs_bias[:, i, :], ALU.mult, ALU.add)
                last.then_inc(emptied[kind], 1)
                dve.wait_ge(emptied[kind], g + 1)

            def residual(kind, g, before):
                dve.wait_ge(filled[kind], g + 1)
                dve.tensor_tensor(xs[:, group(g), :], before[:, group(g), :], tiles_of(kind, g),
                                  ALU.add).then_inc(emptied[kind], 1)
                dve.wait_ge(emptied[kind], g + 1)

            def choose(f, g):
                dve.wait_ge(logits_copied[f], g + 1)
                for t in range(TG):
                    last = dve.max(top[:, f, TG * g + t, :], lg[:, f, g, 0, t, :])
                settled(last)
                settled(dve.memset(top[:, f, group(g), 2:8], LOWEST))
                for t in range(TG):
                    last = dve.match_replace(lg[:, f, g, 1, t, :], top[:, f, TG * g + t, :], lg[:, f, g, 0, t, :],
                                             LOWEST)
                settled(last)
                settled(dve.tensor_tensor(ex[:, f, g, :, :, :], lg[:, f, g, :, :, 0:TRUE],
                                          top[:, f, group(g), 0:1].unsqueeze(1).broadcast_to([P, 2, TG, TRUE]),
                                          ALU.subtract))
                dve.wait_ge(rstd_made[2 * f + 1], g + 1)
                dve.tensor_tensor(ex[:, f, g, :, :, :], ex[:, f, g, :, :, :],
                                  rstd[:, 2 * f + 1, group(g)].unsqueeze(1).unsqueeze(3)
                                  .broadcast_to([P, 2, TG, TRUE]), ALU.mult).then_inc(exp_args[f], 1)

            def weigh(f, g):
                dve.wait_ge(exps_made[f], g + 1)
                t = group(g)
                settled(dve.tensor_tensor(picked[:, f, t, 0:TRUE], ex[:, f, g, 0, :, :], ex[:, f, g, 1, :, :],
                                          ALU.subtract))
                settled(dve.tensor_reduce(den[:, f, t], picked[:, f, t, :], AX.X, ALU.add))
                settled(dve.reciprocal(den[:, f, t], den[:, f, t]))
                settled(dve.tensor_tensor(ew[:, f, t, :], picked[:, f, t, 0:TRUE],
                                          den[:, f, t].unsqueeze(2).broadcast_to([P, TG, TRUE]), ALU.mult))
                dve.wait_ge(filled[f"z{f}"], g + 1)
                dve.tensor_tensor(hz[:, t, :].rearrange("p t (e r) -> p t e r", r=RANK),
                                  z_and_logits(f, g)[:, :, 0:P].rearrange("p t (e r) -> p t e r", r=RANK),
                                  ew[:, f, t, :].unsqueeze(3).broadcast_to([P, TG, TRUE, RANK]), ALU.mult).then_inc(emptied[f"z{f}"], 1)

            for stage, n in ORDER:
                if stage == "stats0":
                    dve.wait_ge(x_in[n], 16)
                    stats(0, n)
                elif stage == "norm2":
                    t = group(n)
                    dve.wait_ge(rstd_made[2], n + 1)
                    settled(dve.scalar_tensor_tensor(nshift[:, t], mv[:, 2, t, 0], -1.0, rstd[:, 2, t],
                                                     ALU.mult, ALU.mult))
                    dve.tensor_scalar(nshift[:, t], nshift[:, t], SHIFT, None, ALU.add).then_inc(nshift_made, 1)
                elif stage == "w_lin":
                    dve.wait_ge(wa_loaded, 64)
                    centre_rows(0, wa_in[:, 0:3, :], wa_centred)
                elif stage == "w_ffn":
                    dve.wait_ge(wf_loaded, 16 * 3)
                    dve.wait_ge(gate_w_loaded, 16)
                    dve.tensor_scalar(wf_in[:, 3, :], wf_in[:, 3, :], LORA_SCALE, None, ALU.mult)
                    centre_rows(1, wf_in[:, 0:3, :], wf_centred)
                elif stage == "feature":
                    feature("q", n, qT, qe, q_made)
                    feature("k", n, k, ke, k_made)
                elif stage == "kxT":
                    dve.wait_ge(emptied["kx"], n + 1)
                    dve.wait_ge(consts_step, 2)
                    dve.tensor_scalar(ksum[:, n, :], same_head[:, 0:P:HD], kx[:, n, P:P + 1], None,
                                      ALU.mult).then_inc(ksum_made, 1)
                elif stage == "kvT":
                    dve.wait_ge(filled["kvT"], n + 1)
                    dve.tensor_tensor(kvT[:, n, :], bank("kvT", n)[:, 0:P], same_head[:, :],
                                      ALU.mult).then_inc(emptied["kvT"], 1)
                elif stage == "den":
                    dve.wait_ge(filled["den"], n + 1)
                    settled(dve.tensor_scalar(rden[:, group(n), :],
                                              bank("den", n)[:, 0:TG * H].rearrange("p (t h) -> p t h", h=H),
                                              DEN_EPS, None, ALU.add))
                    dve.reciprocal(rden[:, group(n), :], rden[:, group(n), :]).then_inc(emptied["den"], 1)
                elif stage == "rden":
                    dve.wait_ge(filled["rden"], n + 1)
                    dve.tensor_tensor(qT[:, group(n), :], qT[:, group(n), :], tiles_of("rden", n),
                                      ALU.mult).then_inc(emptied["rden"], 1)
                elif stage == "lin_out":
                    residual("lin_out", n, xs)
                    stats(1, n)
                elif stage in ("z0", "z1"):
                    choose(int(stage[1]), n)
                elif stage in ("weigh0", "weigh1"):
                    weigh(int(stage[5]), n)
                elif stage == "ffn_out0":
                    residual_scaled(1, "ffn_out0", n)
                    stats(2, n)
                elif stage == "scores":
                    dve.wait_ge(filled["scores"], n + 1)
                    dve.scalar_tensor_tensor(pr[:, group(n), :], tiles_of("scores", n), SCORE_SCALE,
                                             causal[:, None, :].broadcast_to([P, TG, P]),
                                             ALU.mult, ALU.add).then_inc(emptied["scores"], 1)
                    dve.wait_ge(emptied["scores"], n + 1)
                    dve.tensor_reduce(nmax[:, group(n)], pr[:, group(n), :], AX.X, ALU.max,
                                      negate=True).then_inc(nmax_made, 1)
                elif stage == "probs":
                    dve.wait_ge(probs_exp, n + 1)
                    settled(dve.reciprocal(rsum[:, group(n)], rsum[:, group(n)]))
                    for i in range(TG * n, TG * n + TG):
                        last = dve.tensor_scalar(pr[:, i, :], pr[:, i, :], rsum[:, i:i + 1], None, ALU.mult)
                    last.then_inc(probs_made, 1)
                elif stage == "val":
                    for a in range(2):
                        dve.wait_ge(emptied["gate"], 2 * n + a + 1)
                        dve.wait_ge(filled["val"], 2 * n + a + 1)
                        dve.scalar_tensor_tensor(gated[:, a, group(n), :], gate[:, a, group(n), :], 1.0,
                                                 tiles_of("val", 2 * n + a), ALU.add,
                                                 ALU.mult).then_inc(emptied["val"], 1)
                elif stage == "att_out":
                    dve.wait_ge(bias_added[2], n + 1)
                    residual("att_out", n, xs_bias)
                    stats(3, n)
                elif stage == "ffn_out1":
                    residual_scaled(3, "ffn_out1", n)

        @block.tensor
        def _(pe):
            def take(kind, n):
                for before, m in BEFORE[kind, n]:
                    pe.wait_ge(emptied[before], m + 1)
                return bank(kind, n)

            def transposes(kind, g, src):
                dst = take(kind, g)
                for t in range(TG):
                    last = pe.transpose(dst[:, P * t:P * t + P], src(TG * g + t), ident[:, :])
                last.then_inc(filled[kind], 1)

            def wide(kind, n, lhs, rhs):
                pe.matmul(take(kind, n), lhs, rhs, start=True, stop=True).then_inc(filled[kind], 1)

            def by_tile(kind, n, lhs, rhs, width=P, pitch=P):
                dst = take(kind, n)
                for t in range(TG):
                    last = pe.matmul(dst[:, pitch * t:pitch * t + width], lhs(TG * n + t), rhs(TG * n + t),
                                     start=True, stop=True)
                last.then_inc(filled[kind], 1)

            def attention_weights():
                pe.wait_ge(wb_loaded, 16 * 8)
                pe.wait_ge(consts_step, 2)
                dst = take("w_vg", 0)
                pe.matmul(dst, centre[:, :], wb_in[:, 2:4, :], start=True, stop=False)
                pe.matmul(dst, share_row[:, :], bias_row[:, 2:4, :], start=False,
                          stop=True).then_inc(filled["w_vg"], 1)
                dst = take("w_qk", 0)
                for n in range(4):
                    cols, half = dst[:, P * n:P * n + P], slice(P * (n % 2), P * (n % 2) + P)
                    pe.matmul(cols, wb_in[:, n // 2, half], centre[:, :], start=True, stop=False)
                    last = pe.matmul(cols, bias_row[:, n // 2, half], share_row[:, :], start=False, stop=True)
                last.then_inc(filled["w_qk"], 1)
                pe.wait_ge(emptied["w_qk"], 1)
                dst = take("w_m", 0)[:, 0:P]
                pe.matmul(dst, w_qkT[:, 0, :], w_qkT[:, 2, :], start=True, stop=False)
                pe.matmul(dst, w_qkT[:, 1, :], w_qkT[:, 3, :], start=False, stop=True).then_inc(filled["w_m"], 1)

            pe.wait_ge(consts_step, 1)
            for stage, n in ORDER:
                if stage == "w_lin":
                    pe.wait_ge(wa_loaded, 64)
                    pe.wait_ge(wa_centred, 1)
                    transposes("w_lin", 0, lambda i: wa_in[:, i, :])
                    pe.wait_ge(emptied["w_lin"], 1)
                elif stage == "w_ffn":
                    pe.wait_ge(wf_centred, 1)
                    transposes("w_ffn", 0, lambda i: wf_in[:, i, :])
                elif stage == "w_b":
                    attention_weights()
                elif stage in ("xT0", "xT2"):
                    pe.wait_ge(normed[int(stage[2])], n + 1)
                    transposes(stage, n, lambda i: xn[:, i, 0:P])
                elif stage in ("xT1", "xT3"):
                    pe.wait_ge(emptied["lin_out" if stage == "xT1" else "att_out"], n + 1)
                    transposes(stage, n, lambda i: xs[:, i, :])
                elif stage == "qk":
                    pe.wait_ge(emptied["xT0"], n + 1)
                    wide("q", n, wa[:, 0, :], xT[:, group(n), :])
                    by_tile("k", n, lambda i: xT[:, i, :], lambda i: wa[:, 1, :])
                elif stage == "kx":
                    pe.wait_ge(k_made, n + 1)
                    if n % GB == 0:
                        take("kx", n // GB)
                    for i in range(TG * n, TG * n + TG):
                        last = pe.matmul(bank("kx", n // GB)[:, 0:P + 1], k[:, i, :], xn[:, i, :], start=i % TB == 0,
                                         stop=i % TB == TB - 1)
                    if n % GB == GB - 1:
                        last.then_inc(filled["kx"], 1)
                elif stage == "kxT":
                    pe.wait_ge(emptied["kx"], n + 1)
                    pe.transpose(take("kxT", n)[:, 0:P], kx[:, n, 0:P], ident[:, :]).then_inc(filled["kxT"], 1)
                elif stage == "kvT":
                    pe.wait_ge(emptied["kxT"], n + 1)
                    pe.matmul(take("kvT", n)[:, 0:P], wa[:, 2, :], kxT[:, n, :], start=True,
                              stop=True).then_inc(filled["kvT"], 1)
                elif stage == "kvo":
                    pe.wait_ge(emptied["kvT"], n + 1)
                    pe.matmul(take("kvo", n)[:, 0:P], kvT[:, n, :], wa[:, 3, :], start=True,
                              stop=True).then_inc(filled["kvo"], 1)
                elif stage == "den":
                    pe.wait_ge(ksum_made, n // GB + 1)
                    pe.wait_ge(q_made, n + 1)
                    by_tile("den", n, lambda i: qT[:, i, :], lambda i: ksum[:, i // TB, :], width=H, pitch=H)
                elif stage == "rden":
                    pe.wait_ge(rden_widened, n + 1)
                    transposes("rden", n, lambda i: rden_wide[:, i, :])
                elif stage == "lin_out":
                    pe.wait_ge(emptied["kvo"], n // GB + 1)
                    pe.wait_ge(emptied["rden"], n + 1)
                    by_tile("lin_out", n, lambda i: qT[:, i, :], lambda i: kvo[:, i // TB, :])
                elif stage in ("z0", "z1"):
                    f = int(stage[1])
                    pe.wait_ge(emptied["w_ffn"], 1)
                    pe.wait_ge(emptied[f"xT{2 * f + 1}"], n + 1)
                    take(stage, n)
                    for t in range(TG):
                        last = pe.matmul(z_and_logits(f, n)[:, t, 0:P + EXPERTS], xT[:, TG * n + t, :],
                                         wf[:, 0:2, :].rearrange("p a c -> p (a c)")[:, 0:P + EXPERTS],
                                         start=True, stop=True)
                    last.then_inc(filled[stage], 1)
                elif stage in ("hT0", "hT1"):
                    pe.wait_ge(emptied[f"z{stage[2]}"], n + 1)
                    transposes(stage, n, lambda i: hz[:, i, :])
                elif stage in ("ffn_out0", "ffn_out1"):
                    pe.wait_ge(emptied[f"hT{stage[7]}"], n + 1)
                    dst = take(stage, n)
                    for t in range(TG):
                        i, cols = TG * n + t, dst[:, P * t:P * t + P]
                        pe.matmul(cols, xT[:, i, :], wf[:, 2, :], start=True, stop=False)
                        last = pe.matmul(cols, hT[:, i, :], wf[:, 3, :], start=False, stop=True)
                    last.then_inc(filled[stage], 1)
                elif stage == "u":
                    pe.wait_ge(emptied["w_m"], 1)
                    pe.wait_ge(emptied["xT2"], n + 1)
                    wide("u", n, w_m[:, :], xT[:, group(n), :])
                    by_tile("gram", n, lambda i: xn[:, i, 0:P], lambda i: xn[:, i, 0:P])
                elif stage == "scores":
                    pe.wait_ge(emptied["u"], n + 1)
                    by_tile("scores", n, lambda i: uT[:, i, :], lambda i: xT[:, i, :])
                elif stage == "gate":
                    pe.wait_ge(emptied["w_vg"], 1)
                    pe.wait_ge(emptied["xT2"], n + 1)
                    for a in range(2):
                        wide("gate", 2 * n + a, w_vg[:, 1, P * a:P * a + P], xT[:, group(n), :])
                elif stage == "pT":
                    pe.wait_ge(probs_made, n + 1)
                    transposes("pT", n, lambda i: pr[:, i, :])
                elif stage == "wT":
                    pe.wait_ge(emptied["pT"], n + 1)
                    dst = take("wT", n)
                    for t in range(TG):
                        i, cols = TG * n + t, dst[:, P * t:P * t + P]
                        last = pe.matmul(cols, xn[:, i, 0:P], pT[:, i, :], start=True, stop=i % TB == 0)
                        if i % TB:
                            pe.wait_ge(grams_made, grams_before(i))
                            last = pe.matmul(cols, gram[:, i, :], uT[:, i, :], start=False, stop=True)
                    last.then_inc(filled["wT"], 1)
                elif stage == "val":
                    pe.wait_ge(emptied["wT"], n + 1)
                    for a in range(2):
                        wide("val", 2 * n + a, w_vg[:, 0, P * a:P * a + P], wT[:, group(n), :])
                elif stage == "att_out":
                    pe.wait_ge(emptied["val"], 2 * n + 2)
                    dst = take("att_out", n)
                    for t in range(TG):
                        i, cols = TG * n + t, dst[:, P * t:P * t + P]
                        pe.matmul(cols, gated[:, 0, i, :], w_out[:, 0, :], start=True, stop=False)
                        last = pe.matmul(cols, gated[:, 1, i, :], w_out[:, 1, :], start=False, stop=True)
                    last.then_inc(filled["att_out"], 1)


_INS = ["L0_attn_a_x", "L0_attn_a_Wq", "L0_attn_a_Wk", "L0_attn_a_Wv", "L0_attn_a_Wo",
        "L0_attn_b_Wq", "L0_attn_b_bq", "L0_attn_b_Wk", "L0_attn_b_bk", "L0_attn_b_Wv", "L0_attn_b_bv",
        "L0_attn_b_Wg", "L0_attn_b_bg", "L0_attn_b_Wo", "L0_attn_b_bo",
        "L0_ffn_base_w", "L0_ffn_base_b", "L0_ffn_gate_w", "L0_ffn_lora_A", "L0_ffn_lora_B"]


def kernel(**inputs):
    import numpy as np
    import concourse.bacc as bacc
    from concourse.bass_utils import run_bass_kernel_spmd

    nc = bacc.Bacc("TRN2", target_bir_lowering=False, num_devices=1)
    arrays, args = {}, []
    for name in _INS:
        a = np.ascontiguousarray(inputs[name])
        arrays[f"in_{name}"] = a
        args.append(nc.dram_tensor(f"in_{name}", a.shape, mybir.dt.from_np(a.dtype), kind="ExternalInput").ap())
    out = nc.dram_tensor("out", [B, S, P], F32, kind="ExternalOutput").ap()
    hybrid_block(nc, *args, out)
    return run_bass_kernel_spmd(nc, [arrays], core_ids=[0]).results[0]["out"]
```

```python
from contextlib import ExitStack

import concourse.bass as bass
from concourse import mybir

F32 = mybir.dt.float32
ALU = mybir.AluOpType
ACT = mybir.ActivationFunctionType
AX = mybir.AxisListType

P = 128
B, S = 2, 1024
TILES = B * S // P
TG = 4
GROUPS = TILES // TG
GB = GROUPS // B
TB = TILES // B
H = 16
HD = P // H
D = 256
EXPERTS, TRUE, RANK = 10, 8, 16
LORA_SCALE = 2.0
PAD = 16
LOWEST, TINY = -1.0e30, 1.2e-38
LN_EPS, DEN_EPS = 1e-5, 1e-6
SHIFT = 0.125
BIAS_SHARE = 1.0 / (P * SHIFT)
SCORE_SCALE = D ** -0.5
BANKS = 8

ORDER = [(item.split(":")[0], int(item.split(":")[1])) for item in """
stats0:0 norm0:0 stats0:1 xT0:0 w_lin:0 norm0:1 k:0 w_ffn:0 q:0 stats0:2 stats0:3 xT0:1 norm0:2 norm0:3
w_vg:0 w_qk:0 q_feature:0 k:1 k_feature:0 q:1 k_feature:1 kx:0 q_feature:1 xT0:2 kx:1 xT0:3 k:2 q:2 kxT:0
den:0 den:1 widen:0 k:3 q_feature:2 widen:1 kvT:0 k_feature:2 k_feature:3 q:3 rden:0 kvo:0 kx:2 q_feature:3
rden:1 lin_out:0 kx:3 stats1:0 xT1:0 w_out:0 lin_out:1 kxT:1 z0:0 stats1:1 choose0:0 xT1:1 kvT:1 den:2 z0:1
widen:2 choose0:1 args0:0 exps0:0 bias1:0 pick0:0 bias1:1 kvo:1 den:3 rden:2 widen:3 weigh0:0 args0:1
exps0:1 rden:3 lin_out:2 pick0:1 bias1:2 hT0:0 weigh0:1 lin_out:3 ffn_out0:0 stats2:0 w_m:0 xT1:2 xT1:3
hT0:1 stats1:2 z0:2 norm2:0 choose0:2 args0:2 ffn_out0:1 exps0:2 z0:3 pick0:2 xT2:0 stats2:1 weigh0:2
gram:0 u:0 stats1:3 gate:0 hT0:2 norm2:1 choose0:3 args0:3 scores:0 exps0:3 pick0:3 ffn_out0:2 weigh0:3
xT2:1 softmax:0 gate:1 stats2:2 u:1 gate:2 hT0:3 probs:0 gram:1 norm2:2 scores:1 pT:0 softmax:1 ffn_out0:3
bias2:0 grams:0 gram:2 xT2:2 bias1:3 grams:1 probs:1 stats2:3 gate:3 wT:0 gate:4 u:2 val:0 norm2:3 val:1
scores:2 pT:1 att_out:0 stats3:0 softmax:2 xT2:3 probs:2 grams:2 wT:1 xT3:0 u:3 pT:2 gram:3 bias2:1 val:2
gate:5 scores:3 softmax:3 z1:0 val:3 bias3:0 bias2:2 choose1:0 bias2:3 args1:0 probs:3 wT:2 exps1:0
att_out:1 val:4 pick1:0 grams:3 pT:3 gate:6 val:5 weigh1:0 xT3:1 wT:3 z1:1 stats3:1 choose1:1 gate:7 val:6
bias3:1 args1:1 exps1:1 pick1:1 val:7 att_out:2 stats3:2 att_out:3 xT3:2 hT1:0 bias3:2 weigh1:1 z1:2
choose1:2 args1:2 xT3:3 hT1:1 exps1:2 z1:3 pick1:2 stats3:3 choose1:3 args1:3 exps1:3 weigh1:2 pick1:3
weigh1:3 bias3:3 ffn_out1:0 ffn_out1:1 hT1:2 hT1:3 ffn_out1:2 ffn_out1:3
""".split()]

NO_FILLS = {"w_out", "q_feature", "k_feature", "widen", "weigh0", "weigh1", "exps0", "exps1", "softmax",
            "probs", "grams", "choose0", "choose1", "args0", "args1", "pick0", "pick1"}
READ_IN = {"z0": "weigh0", "z1": "weigh1"}
WHEN = {item: at for at, item in enumerate(ORDER)}
FILLS = []
for (stage, n), at in WHEN.items():
    if stage == "kx":
        if n % GB == 0:
            FILLS += [(stage, n // GB, at, WHEN[stage, n + GB - 1])]
    elif stage not in NO_FILLS and not stage.startswith(("stats", "norm", "bias")):
        FILLS.append((stage, n, at, WHEN[READ_IN.get(stage, stage), n]))
KINDS = list(dict.fromkeys(fill[0] for fill in FILLS))
BANK, BEFORE = {}, {}
holder = {}
done = [-BANKS + i for i in range(BANKS)]
for kind, n, at, last in FILLS:
    width = 2 if kind in ("z0", "z1") else 1
    first = min(range(BANKS + 1 - width), key=lambda i: (max(done[i:i + width]), i))
    BANK[kind, n] = first
    BEFORE[kind, n] = list(dict.fromkeys(holder[i] for i in range(first, first + width) if i in holder))
    for i in range(first, first + width):
        holder[i], done[i] = (kind, n), last + len(BANK) / len(FILLS)


INPUT_OF = {1: "lin_out", 2: "ffn_out0", 3: "att_out"}


def hybrid_block(nc, x, a_wq, a_wk, a_wv, a_wo, b_wq, b_bq, b_wk, b_bk, b_wv, b_bv, b_wg, b_bg, b_wo, b_bo,
                 base_w, base_b, gate_w, lora_a, lora_b, out):
    ctx = ExitStack()
    with ctx:
        def sb(name, shape):
            return ctx.enter_context(nc.sbuf_tensor(name, shape, F32))

        def sem(name):
            return ctx.enter_context(nc.semaphore(name))

        wa_in = sb("wa_in", [P, 4, P])
        wa = sb("wa", [P, 4, P])
        wf_in = sb("wf_in", [P, 4, P])
        wf = sb("wf", [P, 4, P])
        base_all = sb("base_all", [P, P])
        off = sb("off", [P, 2, 3])
        wb_in = sb("wb_in", [P, 4, D])
        bias_row = sb("bias_row", [1, 4, D])
        share_row = sb("share_row", [1, P])
        w_vg = sb("w_vg", [P, 2, D])
        w_qkT = sb("w_qkT", [P, 4, P])
        w_m = sb("w_m", [P, P])
        w_out = sb("w_out", [P, 2, P])
        bo_all = sb("bo_all", [P, P])
        ident = sb("ident", [P, P])
        centre = sb("centre", [P, P])
        same_head = sb("same_head", [P, P])
        causal = sb("causal", [P, P])
        half_neg = sb("half_neg", [P, TG])
        warm = sb("warm", [P, 1])

        xs = sb("xs", [P, TILES, P])
        xs_bias = sb("xs_bias", [P, TILES, P])
        xn = sb("xn", [P, TILES, P + 1])
        xT = sb("xT", [P, TILES, P])
        st = sb("st", [P, 4, TILES, 6])
        mv = sb("mv", [P, 4, TILES, 2])
        rstd = sb("rstd", [P, 4, TILES])
        nshift = sb("nshift", [P, TILES])
        qe = sb("qe", [P, TILES, P])
        ke = sb("ke", [P, TILES, P])
        qT = sb("qT", [P, TILES, P])
        k = sb("k", [P, TILES, P])
        kx = sb("kx", [P, B, P + 1])
        kxT = sb("kxT", [P, B, P])
        kvT = sb("kvT", [P, B, P])
        kvo = sb("kvo", [P, B, P])
        ksum = sb("ksum", [P, B, H])
        rden = sb("rden", [P, TILES, H])
        rden_wide = sb("rden_wide", [P, TILES, P])
        lg = sb("lg", [P, 2, GROUPS, 2, TG, PAD])
        top = sb("top", [P, 2, TILES, 8])
        ex = sb("ex", [P, 2, GROUPS, 2, TG, TRUE])
        picked = sb("picked", [P, 2, TILES, TRUE + 1])
        ew = sb("ew", [P, 2, TILES, TRUE])
        den = sb("den", [P, 2, TILES])
        hz = qe
        hT = ke
        uT = qT
        gram_in = sb("gram_in", [P, TILES, P])
        gram = sb("gram", [P, TILES, P])
        pr = sb("pr", [P, TILES, P])
        nmax = sb("nmax", [P, TILES])
        rsum = sb("rsum", [P, TILES])
        pT = sb("pT", [P, TILES, P])
        wT = k
        gate = sb("gate", [P, 2, TILES, P])
        gated = sb("gated", [P, 2, TILES, P])

        ps = ctx.enter_context(nc.psum_tensor("ps", [P, BANKS, 512], F32))

        def bank(kind, n):
            return ps[:, BANK[kind, n], :]

        def tiles_of(kind, n):
            return bank(kind, n).rearrange("p (t c) -> p t c", t=TG)

        def z_and_logits(f, n):
            first = BANK[f"z{f}", n]
            return ps[:, first:first + 2, :].rearrange("p a c -> p (a c)").rearrange("p (t c) -> p t c", t=TG)

        filled = {kind: sem(f"filled_{kind}") for kind in KINDS}
        emptied = {kind: sem(f"emptied_{kind}") for kind in KINDS}
        x_in = [sem(f"x_in{g}") for g in range(GROUPS)]
        wa_loaded = sem("wa_loaded")
        wf_loaded = sem("wf_loaded")
        wb_loaded = sem("wb_loaded")
        wo_loaded = sem("wo_loaded")
        w_out_halved = sem("w_out_halved")
        consts_step = sem("consts_step")
        pads_set = sem("pads_set")
        wf_centred = sem("wf_centred")
        stats_made = [sem(f"stats_made{n}") for n in range(4)]
        normed = [sem(f"normed{n}") for n in range(4)]
        rstd_made = [sem(f"rstd_made{n}") for n in range(4)]
        gate_w_loaded = sem("gate_w_loaded")
        q_made = sem("q_made")
        k_made = sem("k_made")
        ksum_made = sem("ksum_made")
        rden_made = sem("rden_made")
        rden_widened = sem("rden_widened")
        chosen = [sem(f"chosen{f}") for f in range(2)]
        picked_made = [sem(f"picked_made{f}") for f in range(2)]
        logits_copied = [sem(f"logits_copied{f}") for f in range(2)]
        exp_args = [sem(f"exp_args{f}") for f in range(2)]
        exps_made = [sem(f"exps_made{f}") for f in range(2)]
        bias_added = [sem(f"bias_added{n}") for n in range(4)]
        wa_centred = sem("wa_centred")
        grams_made = sem("grams_made")
        nshift_made = sem("nshift_made")
        nmax_made = sem("nmax_made")
        probs_exp = sem("probs_exp")
        probs_made = sem("probs_made")
        stored = sem("stored")
        dve_step = sem("dve_step")
        tile_stats = sem("tile_stats")
        pool_step = sem("pool_step")

        x_tok = x.rearrange("b (t p) d -> p (b t) d", p=P)
        out_tok = out.rearrange("b (t p) d -> p (b t) d", p=P)

        def grams_before(i):
            return i // TB * (TB - 1) + i % TB

        def gram_tiles(g):
            return TG - 1 if g % GB == GB - 1 else TG

        def group(g):
            return slice(TG * g, TG * g + TG)

        block = ctx.enter_context(nc.Block())

        @block.sync
        def _(sp):
            def load_x(g):
                sp.dma_start(xs[:, group(g), :], x_tok[:, group(g), :]).then_inc(x_in[g], 16)

            load_x(0)
            sp.dma_start(wa_in[:, 0, :], a_wq).then_inc(wa_loaded, 16)
            sp.dma_start(wa_in[:, 1, :], a_wk).then_inc(wa_loaded, 16)
            for g in range(1, GROUPS):
                load_x(g)
            sp.dma_start(wf_in[:, 0, :], lora_a.rearrange("e r d -> (e r) d")).then_inc(wf_loaded, 16)
            sp.dma_start(wf_in[:, 2, :], base_w).then_inc(wf_loaded, 16)
            sp.dma_start(wf_in[:, 3, :].rearrange("o (e r) -> o e r", r=RANK),
                         lora_b.rearrange("e o r -> o e r")).then_inc(wf_loaded, 16)
            for n, w in enumerate((b_wq, b_wk, b_wv, b_wg)):
                sp.dma_start(wb_in[:, n, :], w).then_inc(wb_loaded, 16)
            for n, bias in enumerate((b_bq, b_bk, b_bv, b_bg)):
                sp.dma_start(bias_row[:, n, :], bias.rearrange("(a n) -> a n", a=1)).then_inc(wb_loaded, 16)
            for g in range(GROUPS):
                sp.wait_ge(emptied["ffn_out1"], g + 1)
                sp.dma_start(out_tok[:, group(g), :], xs[:, group(g), :]).then_inc(stored, 16)
            sp.wait_ge(stored, 16 * GROUPS)

        @block.gpsimd
        def _(pool):
            steps = [0]

            def settled(ins):
                steps[0] += 1
                ins.then_inc(pool_step, 1)
                pool.wait_ge(pool_step, steps[0])

            settled(pool.memset(ident[:, :], 0.0))
            pool.affine_select(out=ident[:, :], in_=ident[:, :], compare_op=ALU.not_equal, fill=1.0, base=0,
                               pattern=[[-1, P]], channel_multiplier=1).then_inc(consts_step, 1)
            pool.memset(half_neg[:, :], -0.5)
            settled(pool.memset(wf_in[:, 1, :], 0.0))
            pool.dma_start(wf_in[0:EXPERTS, 1, :], gate_w).then_inc(gate_w_loaded, 16)
            pool.memset(xn[:, :, P:P + 1], 1.0)
            pool.memset(same_head[:, :], 1.0)
            settled(pool.memset(causal[:, :], 0.0))

            def inverse_deviation(n, g):
                t = group(g)
                pool.wait_ge(stats_made[n], g + 1)
                settled(pool.tensor_scalar(rstd[:, n, t], mv[:, n, t, 1], LN_EPS, None, ALU.add))
                pool.tensor_tensor(rstd[:, n, t], rstd[:, n, t], half_neg[:, :], ALU.pow).then_inc(rstd_made[n], 1)

            def constants():
                pool.memset(share_row[:, :], BIAS_SHARE)
                pool.memset(picked[:, :, :, TRUE:TRUE + 1], TINY)
                pool.memset(lg[:, :, :, :, :, :], LOWEST).then_inc(pads_set, 1)
                pool.tensor_scalar(centre[:, :], ident[:, :], -1.0 / P, None, ALU.add)
                heads = same_head[:, :].rearrange("p (h c) -> p h c", c=HD)
                pool.affine_select(out=causal[:, :], in_=causal[:, :], compare_op=ALU.is_ge, fill=LOWEST, base=0,
                                   pattern=[[-1, P]], channel_multiplier=1)
                settled(pool.affine_select(out=heads, in_=heads, compare_op=ALU.is_ge, fill=0.0, base=0,
                                           pattern=[[-HD, H], [0, HD]], channel_multiplier=1))
                pool.affine_select(out=heads, in_=heads, compare_op=ALU.is_ge, fill=0.0, base=HD - 1,
                                   pattern=[[HD, H], [0, HD]], channel_multiplier=-1).then_inc(consts_step, 1)
                pool.dma_start(w_out[:, :, :], b_wo.rearrange("(h p) o -> p h o", p=P)).then_inc(wo_loaded, 16)
                pool.dma_start(bo_all[:, :], b_bo.partition_broadcast(P)).then_inc(wo_loaded, 16)
                pool.dma_start(base_all[:, :], base_b.partition_broadcast(P)).then_inc(wo_loaded, 16)

            def add_bias(n, g):
                pool.wait_ge(emptied[INPUT_OF[n]], g + 1)
                bias = bo_all if n == 2 else base_all
                pool.tensor_tensor(xs_bias[:, group(g), :], xs[:, group(g), :],
                                   bias[:, None, :].broadcast_to([P, TG, P]), ALU.add).then_inc(bias_added[n], 1)

            def sum_grams(g):
                pool.wait_ge(emptied["gram"], g + 1)
                for i in range(TG * g, TG * g + TG):
                    if i % TB == 0:
                        pool.tensor_copy(gram[:, i + 1, :], gram_in[:, i, :]).then_inc(grams_made, 1)
                    elif i % TB < TB - 1:
                        pool.wait_ge(grams_made, grams_before(i))
                        pool.tensor_tensor(gram[:, i + 1, :], gram[:, i, :], gram_in[:, i, :],
                                           ALU.add).then_inc(grams_made, 1)

            def exp_arguments(f, g):
                pool.wait_ge(chosen[f], g + 1)
                settled(pool.tensor_tensor(ex[:, f, g, :, :, :], lg[:, f, g, :, :, 0:TRUE],
                                           top[:, f, group(g), 0:1].unsqueeze(1).broadcast_to([P, 2, TG, TRUE]),
                                           ALU.subtract))
                pool.wait_ge(rstd_made[2 * f + 1], g + 1)
                pool.tensor_tensor(ex[:, f, g, :, :, :], ex[:, f, g, :, :, :],
                                   rstd[:, 2 * f + 1, group(g)].unsqueeze(1).unsqueeze(3)
                                   .broadcast_to([P, 2, TG, TRUE]), ALU.mult).then_inc(exp_args[f], 1)

            def pick(f, g):
                pool.wait_ge(exps_made[f], g + 1)
                pool.tensor_tensor(picked[:, f, group(g), 0:TRUE], ex[:, f, g, 0, :, :], ex[:, f, g, 1, :, :],
                                   ALU.subtract).then_inc(picked_made[f], 1)

            for stage, n in ORDER:
                if stage in ("stats0", "stats1", "stats2", "stats3"):
                    inverse_deviation(int(stage[5]), n)
                elif stage in ("args0", "args1"):
                    exp_arguments(int(stage[4]), n)
                elif stage in ("pick0", "pick1"):
                    pick(int(stage[4]), n)
                elif stage == "w_lin":
                    constants()
                elif stage == "w_out":
                    pool.wait_ge(wo_loaded, 48)
                    pool.tensor_scalar(w_out[:, :, :], w_out[:, :, :], 0.5, None, ALU.mult).then_inc(w_out_halved, 1)
                elif stage in ("bias1", "bias2", "bias3"):
                    add_bias(int(stage[4]), n)
                elif stage == "grams":
                    sum_grams(n)

        @block.scalar
        def _(act):
            act.dma_start(wa_in[:, 2, :], a_wv).then_inc(wa_loaded, 16)
            act.dma_start(wa_in[:, 3, :], a_wo).then_inc(wa_loaded, 16)
            act.wait_ge(consts_step, 1)
            act.activation(warm[:, :], ident[:, 0:1], ACT.Exp)

            def copy_out(kind, n, dst, src=None):
                act.wait_ge(filled[kind], n + 1)
                act.activation(dst, tiles_of(kind, n) if src is None else src, ACT.Copy).then_inc(emptied[kind], 1)

            def feature_parts(kind, g, positive, exponential):
                act.wait_ge(filled[kind], g + 1)
                act.activation(positive[:, group(g), :], tiles_of(kind, g), ACT.Relu)
                act.activation(exponential[:, group(g), :], tiles_of(kind, g), ACT.Exp).then_inc(emptied[kind], 1)

            for stage, n in ORDER:
                if stage == "norm0":
                    act.wait_ge(rstd_made[0], n + 1)
                    for i in range(TG * n, TG * n + TG):
                        last = act.activation(xn[:, i, 0:P], xs[:, i, :], ACT.Copy, scale=rstd[:, 0, i:i + 1])
                    last.then_inc(normed[0], 1)
                elif stage == "norm2":
                    act.wait_ge(nshift_made, n + 1)
                    for i in range(TG * n, TG * n + TG):
                        last = act.activation(xn[:, i, 0:P], xs[:, i, :], ACT.Identity, bias=nshift[:, i:i + 1],
                                              scale=rstd[:, 2, i:i + 1])
                    last.then_inc(normed[2], 1)
                elif stage == "w_lin":
                    copy_out("w_lin", 0, wa[:, :, :])
                elif stage == "w_ffn":
                    copy_out("w_ffn", 0, wf[:, :, :])
                elif stage == "w_vg":
                    copy_out("w_vg", 0, w_vg[:, :, :], bank("w_vg", 0).rearrange("p (a e) -> p a e", a=2))
                elif stage == "w_qk":
                    copy_out("w_qk", 0, w_qkT[:, :, :])
                elif stage == "w_m":
                    copy_out("w_m", 0, w_m[:, :], bank("w_m", 0)[:, 0:P])
                elif stage in ("xT0", "xT1", "xT2", "xT3"):
                    copy_out(stage, n, xT[:, group(n), :])
                elif stage == "q":
                    feature_parts("q", n, qT, qe)
                elif stage == "k":
                    feature_parts("k", n, k, ke)
                elif stage == "kx":
                    if n % GB == GB - 1:
                        b = n // GB
                        copy_out("kx", b, kx[:, b, :], bank("kx", b)[:, 0:P + 1])
                elif stage == "kxT":
                    copy_out("kxT", n, kxT[:, n, :], bank("kxT", n)[:, 0:P])
                elif stage == "kvo":
                    copy_out("kvo", n, kvo[:, n, :], bank("kvo", n)[:, 0:P])
                elif stage == "den":
                    act.wait_ge(filled["den"], n + 1)
                    act.activation(rden[:, group(n), :],
                                   bank("den", n)[:, 0:TG * H].rearrange("p (t h) -> p t h", h=H), ACT.Copy,
                                   bias=DEN_EPS).then_inc(emptied["den"], 1)
                elif stage == "widen":
                    act.wait_ge(rden_made, n + 1)
                    act.activation(rden_wide[:, group(n), :].rearrange("p t (h c) -> p (t h) c", c=HD),
                                   rden[:, group(n), :].rearrange("p t h -> p (t h)").unsqueeze(2)
                                   .broadcast_to([P, TG * H, HD]), ACT.Copy).then_inc(rden_widened, 1)
                elif stage in ("z0", "z1"):
                    f = int(stage[1])
                    if f == 0:
                        act.wait_ge(pads_set, 1)
                    act.wait_ge(filled[stage], n + 1)
                    act.activation(lg[:, f, n, 0, :, 0:EXPERTS], z_and_logits(f, n)[:, :, P:P + EXPERTS],
                                   ACT.Copy).then_inc(logits_copied[f], 1)
                elif stage in ("exps0", "exps1"):
                    f = int(stage[4])
                    act.wait_ge(exp_args[f], n + 1)
                    act.activation(ex[:, f, n, :, :, :], ex[:, f, n, :, :, :], ACT.Exp).then_inc(exps_made[f], 1)
                elif stage in ("hT0", "hT1"):
                    copy_out(stage, n, hT[:, group(n), :])
                elif stage == "u":
                    copy_out("u", n, uT[:, group(n), :])
                elif stage == "gram":
                    copy_out("gram", n, gram_in[:, TG * n:TG * n + gram_tiles(n), :],
                             tiles_of("gram", n)[:, 0:gram_tiles(n), :])
                elif stage == "gate":
                    act.wait_ge(filled["gate"], n + 1)
                    act.activation(gate[:, n % 2, group(n // 2), :], tiles_of("gate", n), ACT.Tanh,
                                   scale=0.5).then_inc(emptied["gate"], 1)
                elif stage == "softmax":
                    act.wait_ge(nmax_made, n + 1)
                    for i in range(TG * n, TG * n + TG):
                        last = act.activation(pr[:, i, :], pr[:, i, :], ACT.Exp, bias=nmax[:, i:i + 1],
                                              accum_out=rsum[:, i:i + 1])
                    last.then_inc(probs_exp, 1)
                elif stage == "pT":
                    copy_out("pT", n, pT[:, group(n), :])
                elif stage == "wT":
                    copy_out("wT", n, wT[:, group(n), :])

        @block.vector
        def _(dve):
            steps = [0]
            counted = [0]

            def settled(ins):
                steps[0] += 1
                ins.then_inc(dve_step, 1)
                dve.wait_ge(dve_step, steps[0])

            def stats(n, g):
                for i in range(TG * g, TG * g + TG):
                    dve.bn_stats(st[:, n, i, :], xs[:, i, :]).then_inc(tile_stats, 1)
                    counted[0] += 1
                for t in range(TG):
                    i = TG * g + t
                    dve.wait_ge(tile_stats, counted[0] - TG + t + 1)
                    last = dve.bn_aggr(mv[:, n, i, :], st[:, n, i, :])
                last.then_inc(stats_made[n], 1)

            def centre_rows(n, rows, made):
                settled(dve.tensor_reduce(off[:, n, :], rows, AX.X, ALU.add))
                settled(dve.tensor_scalar(off[:, n, :], off[:, n, :], -1.0 / P, None, ALU.mult))
                dve.tensor_tensor(rows, rows, off[:, n, :].unsqueeze(2).broadcast_to([P, 3, P]),
                                  ALU.add).then_inc(made, 1)

            def feature(kind, g, positive, exponential, made):
                dve.wait_ge(emptied[kind], g + 1)
                dve.scalar_tensor_tensor(positive[:, group(g), :], exponential[:, group(g), :], 1.0,
                                         positive[:, group(g), :], ALU.min, ALU.add).then_inc(made, 1)

            def residual_scaled(n, kind, g):
                dve.wait_ge(filled[kind], g + 1)
                dve.wait_ge(bias_added[n], g + 1)
                for t in range(TG):
                    i = TG * g + t
                    last = dve.scalar_tensor_tensor(xs[:, i, :], tiles_of(kind, g)[:, t, :], rstd[:, n, i:i + 1],
                                                    xs_bias[:, i, :], ALU.mult, ALU.add)
                last.then_inc(emptied[kind], 1)

            def residual(kind, g, before):
                dve.wait_ge(filled[kind], g + 1)
                dve.tensor_tensor(xs[:, group(g), :], before[:, group(g), :], tiles_of(kind, g),
                                  ALU.add).then_inc(emptied[kind], 1)

            def choose(f, g):
                dve.wait_ge(logits_copied[f], g + 1)
                for t in range(TG):
                    last = dve.max(top[:, f, TG * g + t, :], lg[:, f, g, 0, t, :])
                settled(last)
                settled(dve.memset(top[:, f, group(g), 2:8], LOWEST))
                for t in range(TG):
                    last = dve.match_replace(lg[:, f, g, 1, t, :], top[:, f, TG * g + t, :], lg[:, f, g, 0, t, :],
                                             LOWEST)
                last.then_inc(chosen[f], 1)

            def weigh(f, g):
                dve.wait_ge(picked_made[f], g + 1)
                t = group(g)
                settled(dve.tensor_reduce(den[:, f, t], picked[:, f, t, :], AX.X, ALU.add))
                settled(dve.reciprocal(den[:, f, t], den[:, f, t]))
                settled(dve.tensor_tensor(ew[:, f, t, :], picked[:, f, t, 0:TRUE],
                                          den[:, f, t].unsqueeze(2).broadcast_to([P, TG, TRUE]), ALU.mult))
                dve.wait_ge(filled[f"z{f}"], g + 1)
                dve.tensor_tensor(hz[:, t, :].rearrange("p t (e r) -> p t e r", r=RANK),
                                  z_and_logits(f, g)[:, :, 0:P].rearrange("p t (e r) -> p t e r", r=RANK),
                                  ew[:, f, t, :].unsqueeze(3).broadcast_to([P, TG, TRUE, RANK]),
                                  ALU.mult).then_inc(emptied[f"z{f}"], 1)

            for stage, n in ORDER:
                if stage == "stats0":
                    dve.wait_ge(x_in[n], 16)
                    stats(0, n)
                elif stage in ("stats1", "stats2", "stats3"):
                    dve.wait_ge(emptied[INPUT_OF[int(stage[5])]], n + 1)
                    stats(int(stage[5]), n)
                elif stage == "norm2":
                    t = group(n)
                    dve.wait_ge(rstd_made[2], n + 1)
                    settled(dve.scalar_tensor_tensor(nshift[:, t], mv[:, 2, t, 0], -1.0, rstd[:, 2, t],
                                                     ALU.mult, ALU.mult))
                    dve.tensor_scalar(nshift[:, t], nshift[:, t], SHIFT, None, ALU.add).then_inc(nshift_made, 1)
                elif stage == "w_lin":
                    dve.wait_ge(wa_loaded, 64)
                    centre_rows(0, wa_in[:, 0:3, :], wa_centred)
                elif stage == "w_ffn":
                    dve.wait_ge(wf_loaded, 16 * 3)
                    dve.wait_ge(gate_w_loaded, 16)
                    dve.tensor_scalar(wf_in[:, 3, :], wf_in[:, 3, :], LORA_SCALE, None, ALU.mult)
                    centre_rows(1, wf_in[:, 0:3, :], wf_centred)
                elif stage == "q_feature":
                    feature("q", n, qT, qe, q_made)
                elif stage == "k_feature":
                    feature("k", n, k, ke, k_made)
                elif stage == "kxT":
                    dve.wait_ge(emptied["kx"], n + 1)
                    dve.wait_ge(consts_step, 2)
                    dve.tensor_scalar(ksum[:, n, :], same_head[:, 0:P:HD], kx[:, n, P:P + 1], None,
                                      ALU.mult).then_inc(ksum_made, 1)
                elif stage == "kvT":
                    dve.wait_ge(filled["kvT"], n + 1)
                    dve.tensor_tensor(kvT[:, n, :], bank("kvT", n)[:, 0:P], same_head[:, :],
                                      ALU.mult).then_inc(emptied["kvT"], 1)
                elif stage == "den":
                    dve.wait_ge(emptied["den"], n + 1)
                    dve.reciprocal(rden[:, group(n), :], rden[:, group(n), :]).then_inc(rden_made, 1)
                elif stage == "rden":
                    dve.wait_ge(filled["rden"], n + 1)
                    dve.tensor_tensor(qT[:, group(n), :], qT[:, group(n), :], tiles_of("rden", n),
                                      ALU.mult).then_inc(emptied["rden"], 1)
                elif stage == "lin_out":
                    residual("lin_out", n, xs)
                elif stage in ("choose0", "choose1"):
                    choose(int(stage[6]), n)
                elif stage in ("weigh0", "weigh1"):
                    weigh(int(stage[5]), n)
                elif stage == "ffn_out0":
                    residual_scaled(1, "ffn_out0", n)
                elif stage == "scores":
                    dve.wait_ge(filled["scores"], n + 1)
                    dve.scalar_tensor_tensor(pr[:, group(n), :], tiles_of("scores", n), SCORE_SCALE,
                                             causal[:, None, :].broadcast_to([P, TG, P]),
                                             ALU.mult, ALU.add).then_inc(emptied["scores"], 1)
                    dve.wait_ge(emptied["scores"], n + 1)
                    dve.tensor_reduce(nmax[:, group(n)], pr[:, group(n), :], AX.X, ALU.max,
                                      negate=True).then_inc(nmax_made, 1)
                elif stage == "probs":
                    dve.wait_ge(probs_exp, n + 1)
                    settled(dve.reciprocal(rsum[:, group(n)], rsum[:, group(n)]))
                    for i in range(TG * n, TG * n + TG):
                        last = dve.tensor_scalar(pr[:, i, :], pr[:, i, :], rsum[:, i:i + 1], None, ALU.mult)
                    last.then_inc(probs_made, 1)
                elif stage == "val":
                    dve.wait_ge(emptied["gate"], n + 1)
                    dve.wait_ge(filled["val"], n + 1)
                    dve.scalar_tensor_tensor(gated[:, n % 2, group(n // 2), :], gate[:, n % 2, group(n // 2), :], 1.0,
                                             tiles_of("val", n), ALU.add, ALU.mult).then_inc(emptied["val"], 1)
                elif stage == "att_out":
                    dve.wait_ge(bias_added[2], n + 1)
                    residual("att_out", n, xs_bias)
                elif stage == "ffn_out1":
                    residual_scaled(3, "ffn_out1", n)

        @block.tensor
        def _(pe):
            def take(kind, n):
                for before, m in BEFORE[kind, n]:
                    pe.wait_ge(emptied[before], m + 1)
                return bank(kind, n)

            def transposes(kind, g, src):
                dst = take(kind, g)
                for t in range(TG):
                    last = pe.transpose(dst[:, P * t:P * t + P], src(TG * g + t), ident[:, :])
                last.then_inc(filled[kind], 1)

            def wide(kind, n, lhs, rhs):
                pe.matmul(take(kind, n), lhs, rhs, start=True, stop=True).then_inc(filled[kind], 1)

            def by_tile(kind, n, lhs, rhs, width=P, pitch=P, tiles=TG):
                dst = take(kind, n)
                for t in range(tiles):
                    last = pe.matmul(dst[:, pitch * t:pitch * t + width], lhs(TG * n + t), rhs(TG * n + t),
                                     start=True, stop=True)
                last.then_inc(filled[kind], 1)

            pe.wait_ge(consts_step, 1)
            for stage, n in ORDER:
                if stage == "w_lin":
                    pe.wait_ge(wa_loaded, 64)
                    pe.wait_ge(wa_centred, 1)
                    transposes("w_lin", 0, lambda i: wa_in[:, i, :])
                    pe.wait_ge(emptied["w_lin"], 1)
                elif stage == "w_ffn":
                    pe.wait_ge(wf_centred, 1)
                    transposes("w_ffn", 0, lambda i: wf_in[:, i, :])
                elif stage == "w_vg":
                    pe.wait_ge(wb_loaded, 16 * 8)
                    pe.wait_ge(consts_step, 2)
                    dst = take("w_vg", 0)
                    pe.matmul(dst, centre[:, :], wb_in[:, 2:4, :], start=True, stop=False)
                    pe.matmul(dst, share_row[:, :], bias_row[:, 2:4, :], start=False,
                              stop=True).then_inc(filled["w_vg"], 1)
                elif stage == "w_qk":
                    pe.wait_ge(wb_loaded, 16 * 8)
                    pe.wait_ge(consts_step, 2)
                    dst = take("w_qk", 0)
                    for half in range(4):
                        w, rows = half // 2, slice(P * (half % 2), P * (half % 2) + P)
                        cols = dst[:, P * half:P * half + P]
                        pe.matmul(cols, wb_in[:, w, rows], centre[:, :], start=True, stop=False)
                        last = pe.matmul(cols, bias_row[:, w, rows], share_row[:, :], start=False, stop=True)
                    last.then_inc(filled["w_qk"], 1)
                elif stage == "w_m":
                    pe.wait_ge(emptied["w_qk"], 1)
                    dst = take("w_m", 0)[:, 0:P]
                    pe.matmul(dst, w_qkT[:, 0, :], w_qkT[:, 2, :], start=True, stop=False)
                    pe.matmul(dst, w_qkT[:, 1, :], w_qkT[:, 3, :], start=False, stop=True).then_inc(filled["w_m"], 1)
                elif stage in ("xT0", "xT2"):
                    pe.wait_ge(normed[int(stage[2])], n + 1)
                    transposes(stage, n, lambda i: xn[:, i, 0:P])
                elif stage in ("xT1", "xT3"):
                    pe.wait_ge(emptied["lin_out" if stage == "xT1" else "att_out"], n + 1)
                    transposes(stage, n, lambda i: xs[:, i, :])
                elif stage == "q":
                    pe.wait_ge(emptied["xT0"], n + 1)
                    wide("q", n, wa[:, 0, :], xT[:, group(n), :])
                elif stage == "k":
                    pe.wait_ge(emptied["xT0"], n + 1)
                    by_tile("k", n, lambda i: xT[:, i, :], lambda i: wa[:, 1, :])
                elif stage == "kx":
                    pe.wait_ge(k_made, n + 1)
                    if n % GB == 0:
                        take("kx", n // GB)
                    for i in range(TG * n, TG * n + TG):
                        last = pe.matmul(bank("kx", n // GB)[:, 0:P + 1], k[:, i, :], xn[:, i, :], start=i % TB == 0,
                                         stop=i % TB == TB - 1)
                    if n % GB == GB - 1:
                        last.then_inc(filled["kx"], 1)
                elif stage == "kxT":
                    pe.wait_ge(emptied["kx"], n + 1)
                    pe.transpose(take("kxT", n)[:, 0:P], kx[:, n, 0:P], ident[:, :]).then_inc(filled["kxT"], 1)
                elif stage == "kvT":
                    pe.wait_ge(emptied["kxT"], n + 1)
                    pe.matmul(take("kvT", n)[:, 0:P], wa[:, 2, :], kxT[:, n, :], start=True,
                              stop=True).then_inc(filled["kvT"], 1)
                elif stage == "kvo":
                    pe.wait_ge(emptied["kvT"], n + 1)
                    pe.matmul(take("kvo", n)[:, 0:P], kvT[:, n, :], wa[:, 3, :], start=True,
                              stop=True).then_inc(filled["kvo"], 1)
                elif stage == "den":
                    pe.wait_ge(ksum_made, n // GB + 1)
                    pe.wait_ge(q_made, n + 1)
                    by_tile("den", n, lambda i: qT[:, i, :], lambda i: ksum[:, i // TB, :], width=H, pitch=H)
                elif stage == "rden":
                    pe.wait_ge(rden_widened, n + 1)
                    transposes("rden", n, lambda i: rden_wide[:, i, :])
                elif stage == "lin_out":
                    pe.wait_ge(emptied["kvo"], n // GB + 1)
                    pe.wait_ge(emptied["rden"], n + 1)
                    by_tile("lin_out", n, lambda i: qT[:, i, :], lambda i: kvo[:, i // TB, :])
                elif stage in ("z0", "z1"):
                    f = int(stage[1])
                    pe.wait_ge(emptied["w_ffn"], 1)
                    pe.wait_ge(emptied[f"xT{2 * f + 1}"], n + 1)
                    take(stage, n)
                    for t in range(TG):
                        last = pe.matmul(z_and_logits(f, n)[:, t, 0:P + EXPERTS], xT[:, TG * n + t, :],
                                         wf[:, 0:2, :].rearrange("p a c -> p (a c)")[:, 0:P + EXPERTS],
                                         start=True, stop=True)
                    last.then_inc(filled[stage], 1)
                elif stage in ("hT0", "hT1"):
                    pe.wait_ge(emptied[f"z{stage[2]}"], n + 1)
                    transposes(stage, n, lambda i: hz[:, i, :])
                elif stage in ("ffn_out0", "ffn_out1"):
                    pe.wait_ge(emptied[f"hT{stage[7]}"], n + 1)
                    dst = take(stage, n)
                    for t in range(TG):
                        i, cols = TG * n + t, dst[:, P * t:P * t + P]
                        pe.matmul(cols, xT[:, i, :], wf[:, 2, :], start=True, stop=False)
                        last = pe.matmul(cols, hT[:, i, :], wf[:, 3, :], start=False, stop=True)
                    last.then_inc(filled[stage], 1)
                elif stage == "u":
                    pe.wait_ge(emptied["w_m"], 1)
                    pe.wait_ge(emptied["xT2"], n + 1)
                    wide("u", n, w_m[:, :], xT[:, group(n), :])
                elif stage == "gram":
                    pe.wait_ge(normed[2], n + 1)
                    by_tile("gram", n, lambda i: xn[:, i, 0:P], lambda i: xn[:, i, 0:P], tiles=gram_tiles(n))
                elif stage == "scores":
                    pe.wait_ge(emptied["u"], n + 1)
                    by_tile("scores", n, lambda i: uT[:, i, :], lambda i: xT[:, i, :])
                elif stage == "gate":
                    pe.wait_ge(emptied["w_vg"], 1)
                    pe.wait_ge(emptied["xT2"], n // 2 + 1)
                    wide("gate", n, w_vg[:, 1, P * (n % 2):P * (n % 2) + P], xT[:, group(n // 2), :])
                elif stage == "pT":
                    pe.wait_ge(probs_made, n + 1)
                    transposes("pT", n, lambda i: pr[:, i, :])
                elif stage == "wT":
                    pe.wait_ge(emptied["pT"], n + 1)
                    dst = take("wT", n)
                    for t in range(TG):
                        i, cols = TG * n + t, dst[:, P * t:P * t + P]
                        last = pe.matmul(cols, xn[:, i, 0:P], pT[:, i, :], start=True, stop=i % TB == 0)
                        if i % TB:
                            pe.wait_ge(grams_made, grams_before(i))
                            last = pe.matmul(cols, gram[:, i, :], uT[:, i, :], start=False, stop=True)
                    last.then_inc(filled["wT"], 1)
                elif stage == "val":
                    pe.wait_ge(emptied["wT"], n // 2 + 1)
                    wide("val", n, w_vg[:, 0, P * (n % 2):P * (n % 2) + P], wT[:, group(n // 2), :])
                elif stage == "att_out":
                    pe.wait_ge(w_out_halved, 1)
                    pe.wait_ge(emptied["val"], 2 * n + 2)
                    dst = take("att_out", n)
                    for t in range(TG):
                        i, cols = TG * n + t, dst[:, P * t:P * t + P]
                        pe.matmul(cols, gated[:, 0, i, :], w_out[:, 0, :], start=True, stop=False)
                        last = pe.matmul(cols, gated[:, 1, i, :], w_out[:, 1, :], start=False, stop=True)
                    last.then_inc(filled["att_out"], 1)


_INS = ["L0_attn_a_x", "L0_attn_a_Wq", "L0_attn_a_Wk", "L0_attn_a_Wv", "L0_attn_a_Wo",
        "L0_attn_b_Wq", "L0_attn_b_bq", "L0_attn_b_Wk", "L0_attn_b_bk", "L0_attn_b_Wv", "L0_attn_b_bv",
        "L0_attn_b_Wg", "L0_attn_b_bg", "L0_attn_b_Wo", "L0_attn_b_bo",
        "L0_ffn_base_w", "L0_ffn_base_b", "L0_ffn_gate_w", "L0_ffn_lora_A", "L0_ffn_lora_B"]


def kernel(**inputs):
    import numpy as np
    import concourse.bacc as bacc
    from concourse.bass_utils import run_bass_kernel_spmd

    nc = bacc.Bacc("TRN2", target_bir_lowering=False, num_devices=1)
    arrays, args = {}, []
    for name in _INS:
        a = np.ascontiguousarray(inputs[name])
        arrays[f"in_{name}"] = a
        args.append(nc.dram_tensor(f"in_{name}", a.shape, mybir.dt.from_np(a.dtype), kind="ExternalInput").ap())
    out = nc.dram_tensor("out", [B, S, P], F32, kind="ExternalOutput").ap()
    hybrid_block(nc, *args, out)
    return run_bass_kernel_spmd(nc, [arrays], core_ids=[0]).results[0]["out"]
```
